# Optimizing a Trainium2 kernel written in Bass

```python
import numpy as np
import jax
import jax.numpy as jnp

def _softmax(x, axis=-1):
    return jax.nn.softmax(x, axis=axis)

def _gelu(x):
    return jax.nn.gelu(x, approximate=True)

def _silu(x):
    return jax.nn.silu(x)

def _sigmoid(x):
    return jax.nn.sigmoid(x)

def _layernorm(x, axis=-1, eps=1e-05):
    m = jnp.mean(x, axis=axis, keepdims=True)
    v = jnp.var(x, axis=axis, keepdims=True)
    return (x - m) / jnp.sqrt(v + eps)

def _scatter_add(tgt, idx, src, axis=0):
    return tgt.at[idx].add(src)

def _segment_sum(src, seg, n):
    return jax.ops.segment_sum(src, seg, n)
kernel_name = 'mk_macaron_d1_jaxref_r8_15e8fd'

def setup_inputs(seed: int=0):
    np.random.seed(seed)
    _w = jnp.asarray

    def _L0_attn_setup():
        import jax, jax.numpy as jnp
        import numpy as np
        D_MODEL = 128
        N_HEADS = 16
        WINDOW = 32
        SEQ = 512
        BATCH = 1
        NEG_INF = -1e+30
        key = jax.random.key(seed)
        ks = jax.random.split(key, 5)
        scale = 0.02
        inp = {'x': jax.random.normal(ks[0], (BATCH, SEQ, D_MODEL), jnp.float32)}
        for i, name in enumerate(['Wq', 'Wk', 'Wv', 'Wo']):
            inp[name] = jax.random.normal(ks[1 + i], (D_MODEL, D_MODEL), jnp.float32) * scale
        for name in ['bq', 'bk', 'bv', 'bo']:
            inp[name] = jnp.zeros((D_MODEL,), jnp.float32)
        return inp
    _L0_attn_in = _L0_attn_setup()

    def _L0_ffn_setup():
        import jax, jax.numpy as jnp
        import numpy as np
        D_MODEL = 128
        D_FF = 512
        NUM_EXPERTS = 8
        key = jax.random.key(seed)
        ks = jax.random.split(key, 8)
        scale_in = 1.0 / np.sqrt(D_MODEL)
        scale_ff = 1.0 / np.sqrt(D_FF)
        x = jax.random.normal(ks[0], (4, 256, D_MODEL), dtype=jnp.float32)
        gate_w = jax.random.uniform(ks[1], (NUM_EXPERTS, D_MODEL), jnp.float32, -scale_in, scale_in)
        gate_b = jax.random.uniform(ks[2], (NUM_EXPERTS,), jnp.float32, -scale_in, scale_in)
        expert_bias = jnp.zeros((NUM_EXPERTS,), dtype=jnp.float32)
        w1 = jax.random.uniform(ks[3], (NUM_EXPERTS, D_MODEL, D_FF), jnp.float32, -scale_in, scale_in)
        b1 = jax.random.uniform(ks[4], (NUM_EXPERTS, D_FF), jnp.float32, -scale_in, scale_in)
        w2 = jax.random.uniform(ks[5], (NUM_EXPERTS, D_FF, D_MODEL), jnp.float32, -scale_ff, scale_ff)
        b2 = jax.random.uniform(ks[6], (NUM_EXPERTS, D_MODEL), jnp.float32, -scale_ff, scale_ff)
        return {'x': x, 'gate_w': gate_w, 'gate_b': gate_b, 'expert_bias': expert_bias, 'w1': w1, 'b1': b1, 'w2': w2, 'b2': b2}
    _L0_ffn_in = _L0_ffn_setup()
    _d = {'L0_attn_x': _L0_attn_in['x'], 'L0_attn_Wq': _L0_attn_in['Wq'], 'L0_attn_bq': _L0_attn_in['bq'], 'L0_attn_Wk': _L0_attn_in['Wk'], 'L0_attn_bk': _L0_attn_in['bk'], 'L0_attn_Wv': _L0_attn_in['Wv'], 'L0_attn_bv': _L0_attn_in['bv'], 'L0_attn_Wo': _L0_attn_in['Wo'], 'L0_attn_bo': _L0_attn_in['bo'], 'L0_ffn_gate_w': _L0_ffn_in['gate_w'], 'L0_ffn_gate_b': _L0_ffn_in['gate_b'], 'L0_ffn_expert_bias': _L0_ffn_in['expert_bias'], 'L0_ffn_w1': _L0_ffn_in['w1'], 'L0_ffn_b1': _L0_ffn_in['b1'], 'L0_ffn_w2': _L0_ffn_in['w2'], 'L0_ffn_b2': _L0_ffn_in['b2']}
    _x0 = _d['L0_attn_x']
    _d['L0_attn_x'] = jax.random.normal(jax.random.fold_in(jax.random.key(seed), 1), (16, 256, 128), dtype=_x0.dtype)
    del _x0
    return _d

def reference(L0_attn_x, L0_attn_Wq, L0_attn_bq, L0_attn_Wk, L0_attn_bk, L0_attn_Wv, L0_attn_bv, L0_attn_Wo, L0_attn_bo, L0_ffn_gate_w, L0_ffn_gate_b, L0_ffn_expert_bias, L0_ffn_w1, L0_ffn_b1, L0_ffn_w2, L0_ffn_b2):

    def _L0_attn_ref(x, Wq, bq, Wk, bk, Wv, bv, Wo, bo):
        import jax, jax.numpy as jnp
        import numpy as np
        D_MODEL = 128
        N_HEADS = 16
        WINDOW = 32
        SEQ = 512
        BATCH = 1
        NEG_INF = -1e+30
        B, S, D = x.shape
        H = N_HEADS
        hd = D // H
        q = (x @ Wq + bq).reshape(B, S, H, hd).transpose(0, 2, 1, 3)
        k = (x @ Wk + bk).reshape(B, S, H, hd).transpose(0, 2, 1, 3)
        v = (x @ Wv + bv).reshape(B, S, H, hd).transpose(0, 2, 1, 3)
        scale = 1.0 / jnp.sqrt(jnp.asarray(hd, x.dtype))
        scores = jnp.einsum('bhqd,bhkd->bhqk', q, k) * scale
        i = jnp.arange(S)[:, None]
        j = jnp.arange(S)[None, :]
        allowed = (j <= i) & (i - j < WINDOW)
        scores = jnp.where(allowed, scores, NEG_INF)
        attn = jax.nn.softmax(scores, axis=-1)
        out = jnp.einsum('bhqk,bhkd->bhqd', attn, v)
        out = out.transpose(0, 2, 1, 3).reshape(B, S, D)
        return out @ Wo + bo

    def _L0_ffn_ref(x, gate_w, gate_b, expert_bias, w1, b1, w2, b2):
        import jax, jax.numpy as jnp
        import numpy as np
        D_MODEL = 128
        D_FF = 512
        NUM_EXPERTS = 8
        gate_logits = jnp.einsum('bsd,ed->bse', x, gate_w) + gate_b + expert_bias
        top_idx = jnp.argmax(gate_logits, axis=-1)
        out = jnp.zeros_like(x)
        for e in range(NUM_EXPERTS):
            mask = (top_idx == e)[..., None].astype(x.dtype)
            h = jax.nn.relu(jnp.einsum('bsd,df->bsf', x, w1[e]) + b1[e])
            y = jnp.einsum('bsf,fd->bsd', h, w2[e]) + b2[e]
            out = out + mask * y
        return out
    x = L0_attn_x
    x = x + 0.5 * _L0_ffn_ref(_layernorm(x, axis=-1), L0_ffn_gate_w, L0_ffn_gate_b, L0_ffn_expert_bias, L0_ffn_w1, L0_ffn_b1, L0_ffn_w2, L0_ffn_b2)
    x = x + _L0_attn_ref(_layernorm(x, axis=-1), L0_attn_Wq, L0_attn_bq, L0_attn_Wk, L0_attn_bk, L0_attn_Wv, L0_attn_bv, L0_attn_Wo, L0_attn_bo)
    x = x + 0.5 * _L0_ffn_ref(_layernorm(x, axis=-1), L0_ffn_gate_w, L0_ffn_gate_b, L0_ffn_expert_bias, L0_ffn_w1, L0_ffn_b1, L0_ffn_w2, L0_ffn_b2)
    return x

_drawn_inputs = setup_inputs


def setup_inputs(seed=0):
    import zlib

    import numpy as np

    out = dict(_drawn_inputs(seed))
    spreads = {'L0_attn_bq': (0.0, 0.8),
     'L0_attn_bk': (0.0, 0.8),
     'L0_attn_bv': (0.0, 0.301),
     'L0_attn_bo': (0.0, 0.1),
     'L0_ffn_expert_bias': (0.0, 0.1)}
    factors = {'L0_attn_Wq': 8.0, 'L0_attn_Wk': 8.0, 'L0_attn_Wv': 3.79}
    for name, (base, spread) in spreads.items():
        noise = np.random.default_rng([zlib.crc32(name.encode()), seed]).standard_normal(out[name].shape)
        drawn = base * np.exp(spread * noise) if base else spread * noise
        out[name] = jnp.asarray(drawn.astype(out[name].dtype))
    for name, factor in factors.items():
        out[name] = (out[name] * factor).astype(out[name].dtype)
    return out
```

```python
from contextlib import ExitStack

import numpy as np

import concourse.bass as bass
from concourse import mybir

F32 = mybir.dt.float32
BF16 = mybir.dt.bfloat16
I32 = mybir.dt.int32
ALU = mybir.AluOpType
ACT = mybir.ActivationFunctionType
AX = mybir.AxisListType

P = 128
BATCH, SEQ, D = 16, 256, 128
HEADS, HD, WINDOW = 16, 8, 32
EXPERTS, DFF = 8, 512
EPS = 1e-5
NEG = -1e30
TOKENS = BATCH * SEQ
TILES = TOKENS // P
HALF_TILES = TILES // 2
HALF_TOKENS = TOKENS // 2
PAIRS = HALF_TILES // 2
FTILES = (HALF_TOKENS + EXPERTS * (P - 1)) // P
FC = DFF // P
QB = 32
NQB = SEQ // QB
G4 = HEADS // 4
KPAD = QB + SEQ
SCALE = float(HD) ** -0.5
NEWTON = 3
AHEAD = 2

CONSTS = {}
_at = 0
for _name, _n in (("ident", P), ("mask", 512), ("mask_first", 512), ("head_col", 4), ("head_row_bd", P),
                  ("before", P), ("ones", P), ("rank_down", EXPERTS), ("tile_steps", HALF_TILES),
                  ("earlier_expert", EXPERTS * EXPERTS), ("tile_number", FTILES * EXPERTS)):
    CONSTS[_name] = (_at, _n)
    _at += _n
N_CONSTS = _at


def constants():
    c = np.zeros((P, N_CONSTS), np.float32)

    def put(name, a):
        at, n = CONSTS[name]
        c[:, at:at + n] = np.broadcast_to(a, (P, n))

    p = np.arange(P)
    q, k = (p % QB)[:, None], np.arange(2 * QB)[None, :]
    allowed = np.where(k < QB, k > q, k - QB <= q)
    block = np.where(allowed, 0.0, NEG)
    no_previous = np.where(allowed & (k >= QB), 0.0, NEG)
    put("ident", np.eye(P))
    put("mask", np.tile(block, (1, 8)))
    put("mask_first", np.concatenate([np.tile(no_previous, (1, 4)), np.tile(block, (1, 4))], 1))
    put("head_col", (p[:, None] // HD) % 4 == np.arange(4)[None, :])
    put("head_row_bd", (p[None, :] // HD) % 4 == p[:, None] // QB)
    put("before", p[:, None] < p[None, :])
    put("ones", 1.0)
    e = np.arange(EXPERTS)
    put("rank_down", (EXPERTS - e)[None, :])
    put("tile_steps", (P * np.arange(HALF_TILES))[None, :])
    put("earlier_expert", (e[None, :] < e[:, None]).reshape(1, -1))
    put("tile_number", np.repeat(np.arange(FTILES), EXPERTS)[None, :])
    return c


def wait(eng, sem, value):
    if isinstance(value, int) and value <= 0:
        return
    eng.wait_ge(sem, value)


class Chain:

    def __init__(self, eng, sem):
        self.eng, self.sem, self.base, self.k = eng, sem, 0, 0

    def then(self, ins):
        self.k += 1
        ins.then_inc(self.sem, 1)
        self.eng.wait_ge(self.sem, self.base + self.k)

    def enter(self, i, per):
        self.start, self.base, self.k, self.per = self.base + self.k, self.base + self.k + i * per, 0, per

    def leave(self, count):
        assert self.k == self.per, f"{self.k} steps in a loop's body"
        self.base, self.k = self.start + count * self.per, 0


def macaron(nc, x, Wq, bq, Wk, bk, Wv, bv, Wo, bo, gate_w, gate_b, expert_bias, w1, b1, w2, b2, consts, out):
    with ExitStack() as ctx:
        def sb(name, shape, dt=F32):
            return ctx.enter_context(nc.sbuf_tensor(name, shape, dt))

        def sem(name):
            return ctx.enter_context(nc.semaphore(name))

        X = sb("X", [P, TILES, D])
        XN = sb("XN", [P, TILES, D])
        YG = sb("YG", [P, TILES, D])
        W1 = sb("W1", [P, EXPERTS, DFF])
        W2 = sb("W2", [P, EXPERTS, FC, D])
        B1 = sb("B1", [P, EXPERTS, DFF])
        B2 = sb("B2", [P, EXPERTS, D])
        WQ, WK, WV, WO = (sb(n, [P, D]) for n in ("WQ", "WK", "WV", "WO"))
        BQKV = sb("BQKV", [P, 3])
        BO = sb("BO", [P, D])
        GW = sb("GW", [P, EXPERTS])
        GB = sb("GB", [P, 2, EXPERTS])
        C = sb("C", [P, N_CONSTS])

        def const(name):
            at, n = CONSTS[name]
            return C[:, at:at + n]

        ident = const("ident")
        ident_b = sb("ident_b", [P, P], BF16)
        mask_b = sb("mask_b", [P, 512], BF16)
        mask_first_b = sb("mask_first_b", [P, 512], BF16)
        before_b = sb("before_b", [P, P], BF16)
        ones_b = sb("ones_b", [P, P], BF16)
        BQM = sb("BQM", [P, 4])

        GN = sb("GN", [P, 2, 2, D])
        GT = sb("GT", [P, 2 * D])
        L = sb("L", [P, HALF_TILES, EXPERTS])
        L0 = sb("L0", [P, 2, EXPERTS])
        stats = sb("stats", [P, 4, 6])
        mv = sb("mv", [P, 4, 2])
        rs_v = sb("rs_v", [P, 4])
        rs_i = sb("rs_i", [P, 4], I32)
        rs_t = sb("rs_t", [P, 4])
        rstd = sb("rstd", [P, 4])
        r_max = sb("r_max", [P, HALF_TILES])
        r_a = sb("r_a", [P, HALF_TILES, EXPERTS])
        r_b = sb("r_b", [P, HALF_TILES, EXPERTS])
        onehot = sb("onehot", [P, HALF_TILES, EXPERTS], BF16)
        r_cnt = sb("r_cnt", [P, EXPERTS])
        r_steps = sb("r_steps", [P, EXPERTS, HALF_TILES])
        r_tiles = sb("r_tiles", [P, EXPERTS])
        r_pre = sb("r_pre", [P, EXPERTS, EXPERTS])
        r_first = sb("r_first", [P, EXPERTS])
        r_end = sb("r_end", [P, EXPERTS])
        r_ge = sb("r_ge", [P, FTILES, EXPERTS])
        r_et = sb("r_et", [P, FTILES])
        r_slot = sb("r_slot", [P, HALF_TILES])
        slot = [sb(f"slot{r}", [P, HALF_TILES], I32) for r in range(4)]
        expert_of = [sb(f"expert_of{r}", [P, FTILES], I32) for r in range(4)]

        xs = sb("xs", [P, 2, D])
        xT = sb("xT", [P, 2, P])
        hp = sb("hp", [P, 2, DFF])
        hT = sb("hT", [P, 2, FC, P])
        ys = sb("ys", [P, 2, D])
        zeros = sb("zeros", [P, D])

        AN = sb("AN", [P, 2, 2, D])
        AT = sb("AT", [P, 2, SEQ])
        QH = sb("QH", [P, 2, 4, SEQ])
        KG = sb("KG", [P, 2, G4, KPAD])
        VB = sb("VB", [P, 2, NQB, P])
        top = sb("top", [P, 2, 16])
        E = sb("E", [P, 2, 16 * 2 * QB])
        PT = sb("PT", [P, 2, (NQB + 1) * 256])
        rden = sb("rden", [P, SEQ])
        ON = sb("ON", [P, SEQ])
        OT = sb("OT", [P, SEQ])
        OB = sb("OB", [P, 2, D])

        PS = ctx.enter_context(nc.psum_tensor("PS", [P, 8, 512], F32))
        BANK_ACT, BANK_DVE = 6, 7
        ND = (4, 5)
        XT_B, H_B, HT_B, Y_B = (0, 1), (2, 3), (4, 5), (6, 7)

        xs_d = [nc.dram_tensor(f"sorted_x{h}", [FTILES * P, D], F32, kind="Internal").ap() for h in range(2)]
        ys_d = [nc.dram_tensor(f"sorted_y{h}", [FTILES * P, D], F32, kind="Internal").ap() for h in range(2)]

        x_loaded = [sem(f"x_loaded{g}") for g in range(2)]
        w_small = sem("w_small_loaded")
        w_ffn = sem("w_ffn_loaded")
        zeros_ready = sem("zeros_ready")
        pads_zeroed = [sem(f"pads_zeroed{h}") for h in range(2)]
        out_stored = sem("out_stored")
        const_ready = sem("const_ready")
        bufs_zeroed = sem("bufs_zeroed")
        dve_step = sem("dve_step")
        norm_waits = sem("norm_waits")
        dve_phase = sem("dve_phase")
        act_phase = sem("act_phase")
        gn_ready = sem("gn_ready")
        gx_full = sem("gx_full")
        gt_ready = sem("gt_ready")
        gl_full = sem("gl_full")
        gl_done = sem("gl_done")
        oh_ready = sem("onehot_ready")
        rank_full = sem("rank_full")
        route_ready = sem("route_ready")
        scattered = [sem(f"scattered{r}") for r in range(4)]
        gathered = [[sem(f"gathered{r}_{q}") for q in range(4)] for r in range(4)]
        xs_loaded = [sem(f"xs_loaded{s}") for s in range(2)]
        xt_full = sem("ffn_xt_full")
        xt_ready = sem("ffn_xt_ready")
        h_full = sem("ffn_h_full")
        h_added = sem("ffn_h_added")
        ht_full = sem("ffn_ht_full")
        ht_ready = sem("ffn_ht_ready")
        y_full = sem("ffn_y_full")
        y_ready = sem("ffn_y_ready")
        y_stored = [sem(f"y_stored{s}") for s in range(2)]
        an_ready = sem("an_ready")
        at_full = sem("at_full")
        at_ready = sem("at_ready")
        qk_full = sem("qk_full")
        qk_ready = sem("qk_ready")
        v_full = sem("v_full")
        v_ready = sem("v_ready")
        s_full = sem("scores_full")
        s_ready = sem("scores_ready")
        e_ready = sem("exp_ready")
        pt_ready = sem("probs_turned")
        pv_full = sem("pv_full")
        on_ready = sem("normalised_ready")
        ot_ready = sem("ot_ready")
        o_full = sem("o_full")
        o_read = sem("o_read")

        N_SMALL = 12
        block = ctx.enter_context(nc.Block())

        def done(J):
            return AHEAD + J + 1

        def slot_free(J):
            return AHEAD + J - 1

        def loads(I, s, i):
            return (I * ((FTILES + 1 - s) // 2) + i) * 16

        @block.sync
        def _(sp):
            sp.dma_start(C[:], consts).then_inc(w_small, 16)
            x_t = x.rearrange("b s d -> (b s) d").rearrange("(t p) d -> p t d", p=P)
            for h in range(2):
                sp.dma_start(X[:, h * HALF_TILES:(h + 1) * HALF_TILES, :],
                             x_t[:, h * HALF_TILES:(h + 1) * HALF_TILES, :]).then_inc(x_loaded[h], 16)
                if h == 0:
                    for dst, src in ((WQ, Wq), (WK, Wk), (WV, Wv), (WO, Wo)):
                        sp.dma_start(dst[:], src).then_inc(w_small, 16)
                    for c, b in enumerate((bq, bk, bv)):
                        sp.dma_start(BQKV[:, c:c + 1], b.rearrange("(p o) -> p o", o=1)).then_inc(w_small, 16)
                    sp.dma_start(BO[:], bo.partition_broadcast(P)).then_inc(w_small, 16)
                    sp.dma_start(GW[:], gate_w).then_inc(w_small, 16)
                    sp.dma_start(GB[:, 0, :], gate_b.partition_broadcast(P)).then_inc(w_small, 16)
                    sp.dma_start(GB[:, 1, :], expert_bias.partition_broadcast(P)).then_inc(w_small, 16)
            sp.wait_ge(zeros_ready, 1)
            for h in range(2):
                sp.dma_start(xs_d[h].rearrange("(j p) d -> p j d", p=P),
                             zeros[:].unsqueeze(1).broadcast_to([P, FTILES, D])).then_inc(pads_zeroed[h], 16)
            sp.dma_start(W1[:], w1.rearrange("e d f -> d e f")).then_inc(w_ffn, 16)
            sp.dma_start(B1[:], b1.partition_broadcast(P)).then_inc(w_ffn, 16)
            sp.dma_start(B2[:], b2.partition_broadcast(P)).then_inc(w_ffn, 16)
            sp.dma_start(W2[:], w2.rearrange("e (c p) n -> p e c n", p=P)).then_inc(w_ffn, 16)

            def load(I, j, s, i):
                sp.wait_ge(xt_full, slot_free(I * FTILES + j))
                sp.dma_start(xs[:, s, :], xs_d[I % 2][bass.ds(j * P, P), :]).then_inc(xs_loaded[s], 16)

            for I in range(4):
                sp.wait_ge(scattered[I], 16 * HALF_TILES)
                sp.wait_ge(xt_full, done(I * FTILES - 1))
                with sp.Fori(0, FTILES // 2) as i:
                    for s in range(2):
                        load(I, i * 2 + s, s, i)
                load(I, FTILES - 1, 0, FTILES // 2)

            o_t = out.rearrange("b s d -> (b s) d").rearrange("(t p) d -> p t d", p=P)
            for h in range(2):
                for q in range(4):
                    sp.wait_ge(dve_phase, 5 + 4 * h + q)
                    t = h * HALF_TILES + 4 * q
                    sp.dma_start(o_t[:, t:t + 4, :], X[:, t:t + 4, :]).then_inc(out_stored, 16)
            sp.wait_ge(out_stored, 16 * 8)

        @block.gpsimd
        def _(pool):
            pool.memset(zeros[:], 0.0).then_inc(zeros_ready, 1)
            pool.memset(KG[:], 0.0).then_inc(bufs_zeroed, 1)

            def scatter(I):
                pool.wait_ge(route_ready, I + 1)
                pool.wait_ge(gt_ready, AHEAD + PAIRS * (I + 1))
                pool.wait_ge(pads_zeroed[I % 2], 16)
                for t in range(HALF_TILES):
                    pool.indirect_dma_start(
                        out=xs_d[I % 2], out_offset=bass.IndirectOffsetOnAxis(ap=slot[I][:, t:t + 1], axis=0),
                        in_=XN[:, (I % 2) * HALF_TILES + t, :], in_offset=None).then_inc(scattered[I], 16)

            def gather(I):
                for s in range(2):
                    pool.wait_ge(y_stored[s], 16 + loads(I + 1, s, 0))
                for t in range(HALF_TILES):
                    pool.indirect_dma_start(
                        out=YG[:, (I % 2) * HALF_TILES + t, :], out_offset=None, in_=ys_d[I % 2],
                        in_offset=bass.IndirectOffsetOnAxis(ap=slot[I][:, t:t + 1], axis=0)
                    ).then_inc(gathered[I][t // 4], 16)

            for I in (0, 2):
                scatter(I)
                scatter(I + 1)
                gather(I)
                gather(I + 1)

        @block.scalar
        def _(act):
            for c in (xt_ready, ht_ready, gt_ready):
                act.sem_inc(c, AHEAD)

            def gate_turned(G, s, tile):
                act.wait_ge(gn_ready, G + 1)
                nc.scalar.copy(XN[:, bass.ds(tile, 2), :], GN[:, s, :, :])
                act.wait_ge(gx_full, G + 1)
                act.wait_ge(gl_full, AHEAD + G)
                nc.scalar.copy(GT[:], PS[:, BANK_ACT, 0:2 * D]).then_inc(gt_ready, 1)

            def ffn(I):
                def xte(j, s):
                    J = I * FTILES + j
                    act.wait_ge(xt_full, done(J))
                    act.wait_ge(h_full, slot_free(J))
                    nc.scalar.copy(xT[:, s, :], PS[:, XT_B[s], 0:P]).then_inc(xt_ready, 1)

                def hte(j, s):
                    J = I * FTILES + j
                    act.wait_ge(ht_full, done(J))
                    act.wait_ge(y_full, slot_free(J))
                    nc.scalar.activation(hT[:, s].rearrange("p c t -> p (c t)"), PS[:, HT_B[s], :],
                                         ACT.Relu).then_inc(ht_ready, 1)

                def store(j, s):
                    act.wait_ge(y_ready, done(I * FTILES + j))
                    act.dma_start(ys_d[I % 2][bass.ds(j * P, P), :], ys[:, s, :]).then_inc(y_stored[s], 16)

                if I >= 2:
                    for q in range(4):
                        act.wait_ge(gathered[I - 2][q], 64)
                xte(0, 0)
                xte(1, 1)
                hte(0, 0)
                with act.Fori(0, (FTILES - 3) // 2) as i:
                    for k in range(2):
                        j = i * 2 + 1 + k
                        xte(j + 1, k)
                        hte(j, 1 - k)
                        store(j - 1, k)
                for j in (FTILES - 2, FTILES - 1):
                    if j + 1 < FTILES:
                        xte(j + 1, (j + 1) % 2)
                    hte(j, j % 2)
                    store(j - 1, (j - 1) % 2)
                store(FTILES - 1, (FTILES - 1) % 2)
                act.sem_inc(act_phase, 1)

            def at_copy(b, s):
                act.wait_ge(at_full, b + 1)
                wait(act, v_full, 2 * b - 2)
                nc.scalar.copy(AT[:, s, :], PS[:, BANK_ACT, 0:SEQ]).then_inc(at_ready, 1)

            def qk_copy(b, s):
                act.wait_ge(qk_full, b + 1)
                wait(act, s_full, 2 * b - 2)
                for h in range(4):
                    nc.scalar.activation(QH[:, s, h, :], PS[:, BANK_ACT, 0:SEQ], ACT.Identity,
                                         bias=BQM[:, h:h + 1], scale=const("head_col")[:, h:h + 1])
                for g in range(G4):
                    r = slice(32 * g, 32 * g + 32)
                    last = nc.scalar.activation(KG[r, s, g, QB:KPAD], PS[r, BANK_ACT, SEQ:2 * SEQ], ACT.Identity,
                                                bias=BQKV[r, 1:2])
                last.then_inc(qk_ready, 1)

            def exp(b, u):
                act.wait_ge(s_ready, 2 * b + u + 1)
                nc.scalar.activation(E[:, u, :], E[:, u, :], ACT.Exp, scale=SCALE).then_inc(e_ready, 1)

            def ot_bias(b):
                act.wait_ge(on_ready, b + 1)
                wait(act, o_full, b)
                nc.scalar.activation(OT[:], ON[:], ACT.Identity, bias=BQKV[:, 2:3]).then_inc(ot_ready, 1)

            def main(b, s, prev, nxt):
                exp(b, 0)
                if nxt:
                    at_copy(b + 1, 1 - s)
                if prev:
                    ot_bias(b - 1)
                exp(b, 1)
                if nxt:
                    qk_copy(b + 1, 1 - s)
                if prev:
                    gate_turned(TILES // 2 + b - 1, 1 - s, (b - 1) * 2)

            act.wait_ge(const_ready, 1)
            act.wait_ge(bufs_zeroed, 1)
            for h in range(2):
                with act.Fori(0, PAIRS // 2) as i:
                    for s in range(2):
                        gate_turned(i * 2 + h * PAIRS + s, s, i * 4 + h * HALF_TILES + 2 * s)
            act.sem_inc(act_phase, 1)
            ffn(0)
            ffn(1)
            at_copy(0, 0)
            qk_copy(0, 0)
            attention_schedule(act, main)
            ot_bias(BATCH - 1)
            gate_turned(TILES - 1, 1, TILES - 2)
            act.sem_inc(act_phase, 1)
            ffn(2)
            ffn(3)

        @block.vector
        def _(dve):
            chain = Chain(dve, dve_step)
            for c in (h_added, y_ready, gl_done):
                dve.sem_inc(c, AHEAD)
            for s in range(2):
                dve.sem_inc(y_stored[s], 16)
            dve.wait_ge(w_small, 16 * N_SMALL)
            nc.vector.tensor_copy(ident_b[:], ident)
            nc.vector.tensor_copy(mask_b[:], const("mask"))
            nc.vector.tensor_copy(mask_first_b[:], const("mask_first"))
            nc.vector.tensor_copy(before_b[:], const("before"))
            nc.vector.tensor_copy(ones_b[:], const("ones"))
            nc.vector.tensor_scalar(BQM[:], const("head_col"), BQKV[:, 0:1], None, ALU.mult).then_inc(const_ready, 1)

            def layer_norm(pairs):
                tiles = [(src, t, dst) for src, dst in pairs for t in range(2)]
                n = len(tiles)
                dve.sem_inc(norm_waits, 1)
                for k, (src, t, dst) in enumerate(tiles):
                    last = nc.vector.bn_stats(stats[:, k, :], src(t))
                chain.then(last)
                dve.sem_inc(norm_waits, 1)
                for k in range(n):
                    last = nc.vector.bn_aggr(mv[:, k, :], stats[:, k, :])
                chain.then(last)
                v, y, w = rs_v[:, 0:n], rstd[:, 0:n], rs_t[:, 0:n]
                chain.then(nc.vector.tensor_scalar(v, mv[:, 0:n, 1], EPS, None, ALU.add))
                chain.then(nc.vector.tensor_scalar(rs_i[:, 0:n], v.bitcast(I32), 1, None, ALU.logical_shift_right))
                chain.then(nc.vector.tensor_scalar(y.bitcast(I32), rs_i[:, 0:n], -1.0, float(0x5F3759DF),
                                                   ALU.mult, ALU.add))
                for _ in range(NEWTON):
                    chain.then(nc.vector.scalar_tensor_tensor(out=w, in0=y, scalar=-0.5, in1=v,
                                                              op0=ALU.mult, op1=ALU.mult))
                    chain.then(nc.vector.tensor_tensor(w, w, y, ALU.mult))
                    chain.then(nc.vector.scalar_tensor_tensor(out=y, in0=w, scalar=1.5, in1=y,
                                                              op0=ALU.add, op1=ALU.mult))
                for k, (src, t, dst) in enumerate(tiles):
                    last = nc.vector.tensor_scalar(dst[:, t, :], src(t), mv[:, k, 0:1], rstd[:, k:k + 1],
                                                   ALU.subtract, ALU.mult)
                return last

            def x_tile(tile):
                return lambda t: X[:, bass.ds(tile + t, 1), :].rearrange("p o d -> p (o d)")

            def gate_norm(G, s, tile):
                dve.wait_ge(gt_ready, AHEAD + G - 1)
                layer_norm([(x_tile(tile), GN[:, s])]).then_inc(gn_ready, 1)

            def gate_logits(G, tile):
                dve.wait_ge(gl_full, AHEAD + G + 1)
                chain.then(nc.vector.tensor_tensor(
                    L0[:], PS[:, BANK_DVE, 0:2 * EXPERTS].rearrange("p (t e) -> p t e", t=2),
                    GB[:, 0, :].unsqueeze(1).broadcast_to([P, 2, EXPERTS]), ALU.add))
                nc.vector.tensor_tensor(L[:, bass.ds(tile, 2), :], L0[:],
                                        GB[:, 1, :].unsqueeze(1).broadcast_to([P, 2, EXPERTS]),
                                        ALU.add).then_inc(gl_done, 1)

            def route(I):
                shape = [P, HALF_TILES, EXPERTS]
                dve.wait_ge(gl_done, AHEAD + PAIRS * (I + 1))
                chain.then(nc.vector.tensor_reduce(r_max[:], L[:], AX.X, ALU.max))
                chain.then(nc.vector.tensor_tensor(r_a[:], L[:], r_max[:].unsqueeze(2).broadcast_to(shape),
                                                   ALU.is_ge))
                chain.then(nc.vector.tensor_tensor(r_b[:], r_a[:], const("rank_down").unsqueeze(1).broadcast_to(shape),
                                                   ALU.mult))
                chain.then(nc.vector.tensor_reduce(r_max[:], r_b[:], AX.X, ALU.max))
                nc.vector.tensor_tensor(onehot[:], r_b[:], r_max[:].unsqueeze(2).broadcast_to(shape),
                                        ALU.is_equal).then_inc(oh_ready, 1)
                dve.wait_ge(rank_full, I + 1)
                chain.then(nc.vector.tensor_copy(r_cnt[:], PS[:, BANK_DVE, P:P + EXPERTS]))
                chain.then(nc.vector.tensor_tensor(
                    r_steps[:], r_cnt[:].unsqueeze(2).broadcast_to([P, EXPERTS, HALF_TILES]),
                    const("tile_steps").unsqueeze(1).broadcast_to([P, EXPERTS, HALF_TILES]), ALU.is_gt))
                chain.then(nc.vector.tensor_reduce(r_tiles[:], r_steps[:], AX.X, ALU.add))
                chain.then(nc.vector.tensor_tensor(
                    r_pre[:], r_tiles[:].unsqueeze(1).broadcast_to([P, EXPERTS, EXPERTS]),
                    const("earlier_expert").rearrange("p (e f) -> p e f", e=EXPERTS), ALU.mult))
                chain.then(nc.vector.tensor_reduce(r_first[:], r_pre[:], AX.X, ALU.add))
                chain.then(nc.vector.tensor_tensor(r_end[:], r_first[:], r_tiles[:], ALU.add))
                chain.then(nc.vector.scalar_tensor_tensor(
                    out=r_a[:], in0=r_first[:].unsqueeze(1).broadcast_to(shape), scalar=float(P),
                    in1=PS[:, BANK_DVE, 0:P].rearrange("p (t e) -> p t e", e=EXPERTS), op0=ALU.mult, op1=ALU.add))
                chain.then(nc.vector.tensor_tensor(r_b[:], r_a[:], onehot[:], ALU.mult))
                chain.then(nc.vector.tensor_reduce(r_slot[:], r_b[:], AX.X, ALU.add))
                nc.vector.tensor_copy(slot[I][:], r_slot[:])
                chain.then(nc.vector.tensor_tensor(
                    r_ge[:], const("tile_number").rearrange("p (j e) -> p j e", e=EXPERTS),
                    r_end[:].unsqueeze(1).broadcast_to([P, FTILES, EXPERTS]), ALU.is_ge))
                chain.then(nc.vector.tensor_reduce(r_et[:], r_ge[:], AX.X, ALU.add))
                nc.vector.tensor_scalar(expert_of[I][:], r_et[:], float(EXPERTS - 1), None,
                                        ALU.min).then_inc(route_ready, 1)

            def ffn(I):
                def expert(j):
                    return dve.value_load(expert_of[I][0:1, bass.ds(j, 1)], min_val=0, max_val=EXPERTS - 1)

                def add_b1(j, s):
                    J = I * FTILES + j
                    e = expert(j)
                    dve.wait_ge(h_full, done(J))
                    dve.wait_ge(ht_full, slot_free(J))
                    nc.vector.tensor_tensor(hp[:, s, :], PS[:, H_B[s], :],
                                            B1[:, bass.ds(e, 1), :].rearrange("p o f -> p (o f)"),
                                            ALU.add).then_inc(h_added, 1)

                def add_b2(j, s, i):
                    J = I * FTILES + j
                    e = expert(j)
                    dve.wait_ge(y_full, done(J))
                    dve.wait_ge(y_stored[s], 16 + loads(I, s, i))
                    nc.vector.tensor_tensor(ys[:, s, :], PS[:, Y_B[s], 0:D],
                                            B2[:, bass.ds(e, 1), :].rearrange("p o f -> p (o f)"),
                                            ALU.add).then_inc(y_ready, 1)

                add_b1(0, 0)
                with dve.Fori(0, FTILES // 2) as i:
                    for s in range(2):
                        add_b1(i * 2 + s + 1, 1 - s)
                        add_b2(i * 2 + s, s, i)
                add_b2(FTILES - 1, 0, FTILES // 2)

            def add_ffn(tile, n):
                return nc.vector.scalar_tensor_tensor(
                    out=X[:, bass.ds(tile, n), :], in0=YG[:, bass.ds(tile, n), :], scalar=0.5,
                    in1=X[:, bass.ds(tile, n), :], op0=ALU.mult, op1=ALU.add)

            def attn_norm(b, s):
                chain.then(add_ffn(b * 2, 2))
                wait(dve, at_full, b - 1)
                layer_norm([(x_tile(b * 2), AN[:, s])]).then_inc(an_ready, 1)

            def values(b, s, u):
                dve.wait_ge(v_full, 2 * b + u + 1)
                wait(dve, pv_full, b - 1)
                nc.vector.tensor_tensor(
                    VB[:, s, 4 * u:4 * u + 4, :], PS[:, BANK_DVE, :].rearrange("p (k n) -> p k n", k=4),
                    const("head_row_bd").unsqueeze(1).broadcast_to([P, 4, P]), ALU.mult).then_inc(v_ready, 1)

            def softmax(b, u):
                sc = PS[:, 2 * u:2 * u + 2, :].rearrange("p k (m n) -> p (k m) n", n=2 * QB)
                dve.wait_ge(s_full, 2 * b + u + 1)
                chain.then(nc.vector.tensor_reduce(top[:, u, :], sc, AX.X, ALU.max))
                nc.vector.tensor_tensor(E[:, u, :].rearrange("p (m n) -> p m n", n=2 * QB), sc,
                                        top[:, u, :].unsqueeze(2).broadcast_to([P, 16, 2 * QB]),
                                        ALU.subtract).then_inc(s_ready, 1)

            def turn(b, s, u):
                dve.wait_ge(e_ready, 2 * b + u + 1)
                wait(dve, pv_full, b - 1)
                at = 4 * u * 256 + QB
                dst = PT[:, s, :]
                dst = bass.AP(dst.tensor, dst.offset + at, [dst.ap[0], [2 * QB, 16], [256 - QB, 2], [1, QB]])
                nc.vector.transpose(dst, E[:, u, :].rearrange("p (m k n) -> p m k n", k=2, n=QB)).then_inc(pt_ready, 1)

            def normalise(b, s):
                dve.wait_ge(pv_full, b + 1)
                chain.then(nc.vector.reciprocal(rden[:], PS[:, ND[s], SEQ:2 * SEQ]))
                wait(dve, ot_ready, b)
                nc.vector.tensor_tensor(ON[:], PS[:, ND[s], 0:SEQ], rden[:], ALU.mult).then_inc(on_ready, 1)

            def residual(b, s, ahead):
                G = TILES // 2 + b
                dve.wait_ge(o_full, b + 1)
                nc.vector.tensor_tensor(OB[:], PS[:, BANK_DVE, 0:2 * D].rearrange("p (t n) -> p t n", t=2),
                                        BO[:].unsqueeze(1).broadcast_to([P, 2, D]), ALU.add).then_inc(o_read, 1)
                if ahead:
                    add_ffn(b * 2 + 6, 2)
                dve.wait_ge(o_read, b + 1)
                xt = X[:, bass.ds(b * 2, 2), :]
                chain.then(nc.vector.tensor_tensor(xt, xt, OB[:], ALU.add))
                dve.wait_ge(gt_ready, AHEAD + G - 1)
                if ahead:
                    wait(dve, at_full, b + 2)
                    layer_norm([(x_tile(b * 2), GN[:, s]), (x_tile(b * 2 + 6), AN[:, 1 - s])]).then_inc(gn_ready, 1)
                    dve.wait_ge(gn_ready, G + 1)
                    dve.sem_inc(an_ready, 1)
                else:
                    layer_norm([(x_tile(b * 2), GN[:, s])]).then_inc(gn_ready, 1)

            def main(b, s, prev, nxt):
                ahead = not (isinstance(b, int) and b + 2 >= BATCH)
                softmax(b, 0)
                if prev:
                    turn(b - 1, 1 - s, 1)
                    normalise(b - 1, 1 - s)
                softmax(b, 1)
                turn(b, s, 0)
                if prev:
                    residual(b - 1, 1 - s, ahead)
                elif ahead:
                    attn_norm(b + 2, s)
                if nxt:
                    values(b + 1, 1 - s, 0)
                    values(b + 1, 1 - s, 1)
                if prev:
                    gate_logits(TILES // 2 + b - 1, b * 2 - (2 + first_tile[0]))

            first_tile = [0]

            for h in range(2):
                dve.wait_ge(x_loaded[h], 16)
                t0 = h * HALF_TILES
                gate_norm(h * PAIRS, 0, t0)
                with dve.Fori(0, PAIRS // 2 - 1) as i:
                    chain.enter(i, 2 * (STEPS_OF_NORM + 1))
                    for k in range(2):
                        pair = i * 2 + k
                        gate_norm(pair + (h * PAIRS + 1), 1 - k, pair * 2 + (t0 + 2))
                        gate_logits(pair + h * PAIRS, pair * 2)
                    chain.leave(PAIRS // 2 - 1)
                gate_norm((h + 1) * PAIRS - 1, 1, t0 + HALF_TILES - 2)
                for pair in (PAIRS - 2, PAIRS - 1):
                    gate_logits(h * PAIRS + pair, pair * 2)
                route(h)
            dve.sem_inc(dve_phase, 1)
            dve.wait_ge(w_ffn, 64)
            ffn(0)
            ffn(1)
            dve.sem_inc(dve_phase, 1)
            for q in range(4):
                dve.wait_ge(gathered[0][q], 64)
            attn_norm(0, 0)
            attn_norm(1, 1)
            values(0, 0, 0)
            values(0, 0, 1)

            def before_loop(first):
                if first == 2:
                    for q in range(4):
                        dve.wait_ge(gathered[1][q], 64)

            def after(b):
                if b == PAIRS:
                    route(2)
                    dve.sem_inc(dve_phase, 1)
                    first_tile[0] = HALF_TILES

            attention_schedule(dve, main, chain, before_loop, after)
            turn(BATCH - 1, 1, 1)
            normalise(BATCH - 1, 1)
            residual(BATCH - 1, 1, False)
            gate_logits(TILES - 1, HALF_TILES - 2)
            route(3)
            dve.sem_inc(dve_phase, 1)
            ffn(2)
            ffn(3)
            for h in range(2):
                for q in range(4):
                    dve.wait_ge(gathered[2 + h][q], 64)
                    add_ffn(h * HALF_TILES + 4 * q, 4).then_inc(dve_phase, 1)

        @block.tensor
        def _(pe):
            for c in (xt_full, h_full, ht_full, y_full, gl_full):
                pe.sem_inc(c, AHEAD)

            def mm(*a, **k):
                return nc.tensor.matmul(*a, skip_group_check=True, **k)

            def gate_turn(G, s):
                pe.wait_ge(gn_ready, G + 1)
                pe.wait_ge(gt_ready, AHEAD + G)
                for t in range(2):
                    last = nc.tensor.transpose(PS[:, BANK_ACT, t * P:(t + 1) * P], GN[:, s, t, :], ident)
                last.then_inc(gx_full, 1)

            def gate_mm(G):
                pe.wait_ge(gt_ready, AHEAD + G + 1)
                pe.wait_ge(gl_done, AHEAD + G)
                for t in range(2):
                    last = mm(PS[:, BANK_DVE, t * EXPERTS:(t + 1) * EXPERTS], GT[:, t * P:(t + 1) * P], GW[:],
                              start=True, stop=True)
                last.then_inc(gl_full, 1)

            def route(I):
                pe.wait_ge(oh_ready, I + 1)
                pe.wait_ge(gl_done, AHEAD + PAIRS * (I + 1))
                oh = onehot[:].rearrange("p t e -> p (t e)")
                mm(PS[:, BANK_DVE, 0:P], before_b[:], oh, start=True, stop=False)
                for k in range(1, HALF_TILES):
                    mm(PS[:, BANK_DVE, k * EXPERTS:P], ones_b[:], oh[:, 0:P - k * EXPERTS], start=False, stop=False)
                for k in range(HALF_TILES):
                    last = mm(PS[:, BANK_DVE, P:P + EXPERTS], ones_b[:], oh[:, k * EXPERTS:(k + 1) * EXPERTS],
                              start=False, stop=(k == HALF_TILES - 1))
                last.then_inc(rank_full, 1)

            def ffn(I):
                def expert(j):
                    return pe.value_load(expert_of[I][0:1, bass.ds(j, 1)], min_val=0, max_val=EXPERTS - 1)

                def turn_x(j, s, i):
                    J = I * FTILES + j
                    pe.wait_ge(xs_loaded[s], 16 + loads(I, s, i))
                    pe.wait_ge(xt_ready, slot_free(J))
                    nc.tensor.transpose(PS[:, XT_B[s], 0:P], xs[:, s, :], ident).then_inc(xt_full, 1)

                def up(j, s):
                    J = I * FTILES + j
                    e = expert(j)
                    pe.wait_ge(xt_ready, done(J))
                    pe.wait_ge(h_added, slot_free(J))
                    mm(PS[:, H_B[s], :], xT[:, s, :], W1[:, bass.ds(e, 1), :].rearrange("p o f -> p (o f)"),
                       start=True, stop=True).then_inc(h_full, 1)

                def turn_h(j, s):
                    J = I * FTILES + j
                    pe.wait_ge(h_added, done(J))
                    pe.wait_ge(ht_ready, slot_free(J))
                    for c in range(FC):
                        last = nc.tensor.transpose(PS[:, HT_B[s], c * P:(c + 1) * P], hp[:, s, c * P:(c + 1) * P],
                                                   ident)
                    last.then_inc(ht_full, 1)

                def down(j, s):
                    J = I * FTILES + j
                    e = expert(j)
                    pe.wait_ge(ht_ready, done(J))
                    pe.wait_ge(y_ready, slot_free(J))
                    for c in range(FC):
                        last = mm(PS[:, Y_B[s], 0:D], hT[:, s, c, :],
                                  W2[:, bass.ds(e, 1), c, :].rearrange("p o n -> p (o n)"),
                                  start=(c == 0), stop=(c == FC - 1))
                    last.then_inc(y_full, 1)

                pe.wait_ge(route_ready, I + 1)
                turn_x(0, 0, 0)
                up(0, 0)
                with pe.Fori(0, FTILES // 2) as i:
                    for s in range(2):
                        j = i * 2 + s
                        turn_x(j + 1, 1 - s, i + s)
                        turn_h(j, s)
                        up(j + 1, 1 - s)
                        down(j, s)
                turn_h(FTILES - 1, 0)
                down(FTILES - 1, 0)

            def turn_a(b, s):
                pe.wait_ge(an_ready, b + 1)
                wait(pe, gt_ready, AHEAD + TILES // 2 + b - 2)
                for t in range(2):
                    last = nc.tensor.transpose(PS[:, BANK_ACT, t * P:(t + 1) * P], AN[:, s, t, :], ident)
                last.then_inc(at_full, 1)

            def project_qk(b, s):
                pe.wait_ge(at_ready, b + 1)
                mm(PS[:, BANK_ACT, 0:SEQ], WQ[:], AT[:, s, :], start=True, stop=True)
                mm(PS[:, BANK_ACT, SEQ:2 * SEQ], WK[:], AT[:, s, :], start=True, stop=True).then_inc(qk_full, 1)

            def project_v(b, s, u, bank_free):
                pe.wait_ge(at_ready, b + 1)
                bank_free()
                for k in range(4):
                    tok = QB * (4 * u + k)
                    for r in range(4):
                        last = mm(PS[32 * r:32 * r + 32, BANK_DVE, k * P:(k + 1) * P], AT[:, s, tok:tok + QB], WV[:],
                                  start=True, stop=True)
                last.then_inc(v_full, 1)

            def scores(b, s, u):
                pe.wait_ge(qk_ready, b + 1)
                wait(pe, s_ready, 2 * b + u - 1)
                for k in range(2):
                    mask = mask_first_b if u == 0 and k == 0 else mask_b
                    mm(PS[:, 2 * u + k, :], ident_b[:], mask[:], start=True, stop=False)
                    for c in range(2):
                        q = QB * (4 * u + 2 * k + c)
                        for h in range(4):
                            last = mm(PS[32 * h:32 * h + 32, 2 * u + k, 256 * c:256 * c + 256],
                                      QH[:, s, h, q:q + QB], KG[:, s, :, q:q + 2 * QB], start=False, stop=True)
                last.then_inc(s_full, 1)

            def weigh(b, s, u):
                pe.wait_ge(pt_ready, 2 * b + u + 1)
                pe.wait_ge(v_ready, 2 * b + 2)
                if u == 0:
                    wait(pe, on_ready, b - 1)
                for kb in (range(3) if u == 0 else range(3, NQB)):
                    n = min(2 * QB, SEQ - kb * QB)
                    for g in range(G4):
                        rhs = PT[:, s, (kb + 1) * 256 + g * 64:(kb + 1) * 256 + g * 64 + n]
                        r = slice(32 * g, 32 * g + 32)
                        mm(PS[r, ND[s], kb * QB:kb * QB + n], VB[:, s, kb, r], rhs, start=(kb == 0), stop=False)
                        last = mm(PS[r, ND[s], SEQ + kb * QB:SEQ + kb * QB + n], bd_ones(g), rhs, start=False,
                                  stop=True)
                if u == 1:
                    last.then_inc(pv_full, 1)

            def bd_ones(g):
                return const("head_row_bd")[:, 32 * g:32 * g + 32]

            def project_o(b):
                pe.wait_ge(ot_ready, b + 1)
                wait(pe, gl_done, AHEAD + TILES // 2 + b - 1)
                pe.wait_ge(v_ready, 2 * b + 4 if not (isinstance(b, int) and b == BATCH - 1) else 2 * BATCH)
                for t in range(2):
                    last = mm(PS[:, BANK_DVE, t * D:(t + 1) * D], OT[:, t * P:(t + 1) * P], WO[:],
                              start=True, stop=True)
                last.then_inc(o_full, 1)

            def main(b, s, prev, nxt):
                scores(b, s, 0)
                if prev:
                    weigh(b - 1, 1 - s, 1)
                if nxt:
                    turn_a(b + 1, 1 - s)
                scores(b, s, 1)
                if nxt:
                    project_qk(b + 1, 1 - s)
                if prev:
                    project_o(b - 1)
                weigh(b, s, 0)
                if nxt:
                    project_v(b + 1, 1 - s, 0, lambda: wait(pe, o_read, b) if prev else pe.wait_ge(v_ready, 2))
                if prev:
                    pe.wait_ge(qk_ready, b + 2 if nxt else BATCH)
                    gate_turn(TILES // 2 + b - 1, 1 - s)
                if nxt:
                    project_v(b + 1, 1 - s, 1, lambda: pe.wait_ge(v_ready, 2 * b + 3))
                if prev:
                    pe.wait_ge(v_ready, 2 * b + 4 if nxt else 2 * BATCH)
                    pe.wait_ge(o_read, b)
                    gate_mm(TILES // 2 + b - 1)

            pe.wait_ge(w_small, 16 * N_SMALL)
            pe.wait_ge(const_ready, 1)
            for h in range(2):
                with pe.Fori(0, PAIRS // 2) as i:
                    for s in range(2):
                        gate_turn(i * 2 + h * PAIRS + s, s)
                        gate_mm(i * 2 + h * PAIRS + s)
                route(h)
            pe.wait_ge(w_ffn, 64)
            pe.wait_ge(act_phase, 1)
            pe.wait_ge(dve_phase, 1)
            ffn(0)
            ffn(1)
            pe.wait_ge(act_phase, 3)
            pe.wait_ge(dve_phase, 2)
            turn_a(0, 0)
            project_qk(0, 0)
            project_v(0, 0, 0, lambda: None)
            project_v(0, 0, 1, lambda: pe.wait_ge(v_ready, 1))

            def after(b):
                if b == PAIRS:
                    route(2)
                    pe.wait_ge(dve_phase, 3)

            attention_schedule(pe, main, after=after)
            weigh(BATCH - 1, 1, 1)
            project_o(BATCH - 1)
            gate_turn(TILES - 1, 1)
            pe.wait_ge(o_read, BATCH)
            gate_mm(TILES - 1)
            route(3)
            pe.wait_ge(act_phase, 4)
            pe.wait_ge(dve_phase, 4)
            ffn(2)
            ffn(3)


def attention_schedule(eng, main, chain=None, before_loop=lambda first: None, after=lambda b: None):
    def straight(b):
        main(b, b % 2, prev=b > 0, nxt=b + 1 < BATCH)
        after(b)

    def loop(first, end):
        before_loop(first)
        count = (end - first) // 2
        with eng.Fori(0, count) as i:
            if chain:
                chain.enter(i, 2 * STEPS_OF_MAIN)
            for s in range(2):
                main(i * 2 + (first + s), s, prev=True, nxt=True)
            if chain:
                chain.leave(count)

    straight(0)
    straight(1)
    loop(2, 8)
    straight(8)
    straight(9)
    loop(10, 14)
    straight(14)
    straight(15)


STEPS_OF_NORM = 5 + 3 * NEWTON
STEPS_OF_MAIN = STEPS_OF_NORM + 5


_INS = ["L0_attn_x", "L0_attn_Wq", "L0_attn_bq", "L0_attn_Wk", "L0_attn_bk", "L0_attn_Wv", "L0_attn_bv",
        "L0_attn_Wo", "L0_attn_bo", "L0_ffn_gate_w", "L0_ffn_gate_b", "L0_ffn_expert_bias", "L0_ffn_w1",
        "L0_ffn_b1", "L0_ffn_w2", "L0_ffn_b2"]


def kernel(**inputs):
    import concourse.bacc as bacc
    from concourse.bass_utils import run_bass_kernel_spmd

    nc = bacc.Bacc("TRN2", target_bir_lowering=False, num_devices=1)
    arrays, args = {}, []
    for name, a in [(n, inputs[n]) for n in _INS] + [("constants", constants())]:
        a = np.ascontiguousarray(np.asarray(a).T if name == "L0_ffn_gate_w" else a)
        arrays[f"in_{name}"] = a
        args.append(nc.dram_tensor(f"in_{name}", a.shape, mybir.dt.from_np(a.dtype), kind="ExternalInput").ap())
    args.append(nc.dram_tensor("out_x", (BATCH, SEQ, D), F32, kind="ExternalOutput").ap())
    macaron(nc, *args)
    r = run_bass_kernel_spmd(nc, [arrays], core_ids=[0])
    return r.results[0]["out_x"]
```

```python
from contextlib import ExitStack

import numpy as np

import concourse.bass as bass
from concourse import mybir

F32 = mybir.dt.float32
BF16 = mybir.dt.bfloat16
I32 = mybir.dt.int32
ALU = mybir.AluOpType
ACT = mybir.ActivationFunctionType
AX = mybir.AxisListType

P = 128
BATCH, SEQ, D = 16, 256, 128
HEADS, HD, WINDOW = 16, 8, 32
EXPERTS, DFF = 8, 512
EPS = 1e-5
NEG = -1e30
TOKENS = BATCH * SEQ
TILES = TOKENS // P
HALF_TILES = TILES // 2
HALF_TOKENS = TOKENS // 2
PAIRS = HALF_TILES // 2
FTILES = (HALF_TOKENS + EXPERTS * (P - 1)) // P
FPAIRS = FTILES // 2
EBITS = 3
EDIGITS = 24 // EBITS
EWORDS = -(-FTILES // EDIGITS)
FC = DFF // P
QB = 32
NQB = SEQ // QB
G4 = HEADS // 4
KPAD = QB + SEQ
SCALE = float(HD) ** -0.5
AHEAD = 2

CONSTS = {}
_at = 0
for _name, _n in (("ident", P), ("mask", 512), ("mask_first", 512), ("head_col", 4), ("head_row_bd", P),
                  ("before", P), ("ones", P), ("rank_down", EXPERTS), ("tile_steps", HALF_TILES),
                  ("earlier_expert", EXPERTS * EXPERTS), ("tile_number", EWORDS * EDIGITS * EXPERTS), ("digit", EDIGITS)):
    CONSTS[_name] = (_at, _n)
    _at += _n
N_CONSTS = _at


def constants():
    c = np.zeros((P, N_CONSTS), np.float32)

    def put(name, a):
        at, n = CONSTS[name]
        c[:, at:at + n] = np.broadcast_to(a, (P, n))

    p = np.arange(P)
    q, k = (p % QB)[:, None], np.arange(2 * QB)[None, :]
    allowed = np.where(k < QB, k > q, k - QB <= q)
    block = np.where(allowed, 0.0, NEG)
    no_previous = np.where(allowed & (k >= QB), 0.0, NEG)
    put("ident", np.eye(P))
    put("mask", np.tile(block, (1, 8)))
    put("mask_first", np.concatenate([np.tile(no_previous, (1, 4)), np.tile(block, (1, 4))], 1))
    put("head_col", (p[:, None] // HD) % 4 == np.arange(4)[None, :])
    put("head_row_bd", (p[None, :] // HD) % 4 == p[:, None] // QB)
    put("before", p[:, None] < p[None, :])
    put("ones", 1.0)
    e = np.arange(EXPERTS)
    put("rank_down", (EXPERTS - e)[None, :])
    put("tile_steps", (P * np.arange(HALF_TILES))[None, :])
    put("earlier_expert", (e[None, :] < e[:, None]).reshape(1, -1))
    put("tile_number", np.repeat(np.arange(EWORDS * EDIGITS), EXPERTS)[None, :])
    put("digit", (float(EXPERTS) ** np.arange(EDIGITS))[None, :])
    return c


def wait(eng, sem, value):
    if isinstance(value, int) and value <= 0:
        return
    eng.wait_ge(sem, value)


class Experts:

    def __init__(self, eng, name):
        self.eng = eng
        self.words = [eng.alloc_register(f"{name}_experts{w}") for w in range(EWORDS)]
        self.moved = eng.alloc_register(f"{name}_moved")

    def load(self, table):
        for w, word in enumerate(self.words):
            self.eng.reg_load(word, table[0:1, w:w + 1])

    def next(self, k):
        e = (self.eng.snap(self.words[0]) // EXPERTS ** k) % EXPERTS
        return self.eng.snap(e, min_val=0, max_val=EXPERTS - 1)

    def passed(self, n):
        bits = EBITS * n
        for w, word in enumerate(self.words):
            self.eng.reg_alu(word, word, bits, ALU.logical_shift_right)
            if w + 1 < EWORDS:
                self.eng.reg_alu(self.moved, self.words[w + 1], (1 << bits) - 1, ALU.bitwise_and)
                self.eng.reg_alu(self.moved, self.moved, EBITS * EDIGITS - bits, ALU.logical_shift_left)
                self.eng.reg_alu(word, word, self.moved, ALU.add)


class Chain:

    def __init__(self, eng, sem):
        self.eng, self.sem, self.base, self.k = eng, sem, 0, 0

    def then(self, ins):
        self.k += 1
        ins.then_inc(self.sem, 1)
        self.eng.wait_ge(self.sem, self.base + self.k)

    def enter(self, i, per):
        self.start, self.base, self.k, self.per = self.base + self.k, self.base + self.k + i * per, 0, per

    def leave(self, count):
        assert self.k == self.per, f"{self.k} steps in a loop's body"
        self.base, self.k = self.start + count * self.per, 0


def macaron(nc, x, Wq, bq, Wk, bk, Wv, bv, Wo, bo, gate_w, gate_b, expert_bias, w1, b1, w2, b2, consts, out):
    with ExitStack() as ctx:
        def sb(name, shape, dt=F32):
            return ctx.enter_context(nc.sbuf_tensor(name, shape, dt))

        def sem(name):
            return ctx.enter_context(nc.semaphore(name))

        X = sb("X", [P, TILES, D])
        XN = sb("XN", [P, TILES, D])
        YG = sb("YG", [P, TILES, D])
        W1 = sb("W1", [P, EXPERTS, DFF])
        W2 = sb("W2", [P, EXPERTS, FC, D])
        B1 = sb("B1", [P, EXPERTS, DFF])
        B2 = sb("B2", [P, EXPERTS, D])
        WQ, WK, WV, WO = (sb(n, [P, D]) for n in ("WQ", "WK", "WV", "WO"))
        BQKV = sb("BQKV", [P, 3])
        BO = sb("BO", [P, D])
        GW = sb("GW", [P, EXPERTS])
        GB = sb("GB", [P, 2, EXPERTS])
        C = sb("C", [P, N_CONSTS])

        def const(name):
            at, n = CONSTS[name]
            return C[:, at:at + n]

        ident = const("ident")
        ident_b = sb("ident_b", [P, P], BF16)
        mask_b = sb("mask_b", [P, 512], BF16)
        mask_first_b = sb("mask_first_b", [P, 512], BF16)
        before_b = sb("before_b", [P, P], BF16)
        ones_b = sb("ones_b", [P, P], BF16)
        BQM = sb("BQM", [P, 4])

        GN = sb("GN", [P, 2, 2, D])
        GT = sb("GT", [P, 2 * D])
        L = sb("L", [P, TILES, EXPERTS])
        L0 = sb("L0", [P, 2, EXPERTS])
        stats = sb("stats", [P, HALF_TILES, 6])
        mv = sb("mv", [P, HALF_TILES, 2])
        var_eps = sb("var_eps", [P, HALF_TILES])
        rstd = sb("rstd", [P, HALF_TILES])
        eps = sb("eps", [P, HALF_TILES])
        minus_half = sb("minus_half", [P, HALF_TILES])
        r_max = sb("r_max", [P, HALF_TILES])
        r_a = sb("r_a", [P, HALF_TILES, EXPERTS])
        r_b = sb("r_b", [P, HALF_TILES, EXPERTS])
        onehot = sb("onehot", [P, HALF_TILES, EXPERTS], BF16)
        r_cnt = sb("r_cnt", [P, EXPERTS])
        r_steps = sb("r_steps", [P, EXPERTS, HALF_TILES])
        r_tiles = sb("r_tiles", [P, EXPERTS])
        r_pre = sb("r_pre", [P, EXPERTS, EXPERTS])
        r_first = sb("r_first", [P, EXPERTS])
        r_end = sb("r_end", [P, EXPERTS])
        r_ge = sb("r_ge", [P, EWORDS * EDIGITS, EXPERTS])
        r_et = sb("r_et", [P, EWORDS * EDIGITS])
        r_slot = sb("r_slot", [P, HALF_TILES])
        slot = [sb(f"slot{r}", [P, HALF_TILES], I32) for r in range(4)]
        r_digits = sb("r_digits", [P, EWORDS, EDIGITS])
        r_words = sb("r_words", [P, EWORDS])
        experts_of = [sb(f"experts_of{r}", [P, EWORDS], I32) for r in range(4)]

        xs = sb("xs", [P, 2, D])
        xT = sb("xT", [P, 2, P])
        hp = sb("hp", [P, 2, DFF])
        hT = sb("hT", [P, 2, FC, P])
        ys = sb("ys", [P, 2, D])
        zeros = sb("zeros", [P, D])

        AN = sb("AN", [P, 2, 2, D])
        AT = sb("AT", [P, 2, SEQ])
        QH = sb("QH", [P, 2, 4, SEQ])
        KG = sb("KG", [P, 2, G4, KPAD])
        VB = sb("VB", [P, 2, NQB, P])
        top = sb("top", [P, 2, 16])
        E = sb("E", [P, 2, 16 * 2 * QB])
        PT = sb("PT", [P, 2, (NQB + 1) * 256])
        rden = sb("rden", [P, SEQ])
        ON = sb("ON", [P, SEQ])
        OT = sb("OT", [P, SEQ])

        PS = ctx.enter_context(nc.psum_tensor("PS", [P, 8, 512], F32))
        BANK_ACT, BANK_DVE = 6, 7
        ND = (4, 5)
        XT_B, H_B, HT_B, Y_B = (0, 1), (2, 3), (4, 5), (6, 7)

        xs_d = [nc.dram_tensor(f"sorted_x{h}", [FTILES * P, D], F32, kind="Internal").ap() for h in range(2)]
        ys_d = [nc.dram_tensor(f"sorted_y{h}", [FTILES * P, D], F32, kind="Internal").ap() for h in range(2)]

        x_loaded = [sem(f"x_loaded{g}") for g in range(2)]
        w_small = sem("w_small_loaded")
        w_ffn = sem("w_ffn_loaded")
        w2_halved = sem("w2_halved")
        zeros_ready = sem("zeros_ready")
        pads_zeroed = [sem(f"pads_zeroed{h}") for h in range(2)]
        out_stored = sem("out_stored")
        const_ready = sem("const_ready")
        bufs_zeroed = sem("bufs_zeroed")
        dve_step = sem("dve_step")
        norm_waits = sem("norm_waits")
        pool_step = sem("pool_step")
        mv_ready = sem("mean_var_ready")
        rstd_ready = sem("rstd_ready")
        pool_waits = sem("pool_waits")
        x_mid = sem("x_after_ffn")
        bo_added = sem("bo_added")
        dve_phase = sem("dve_phase")
        act_phase = sem("act_phase")
        gn_ready = sem("gn_ready")
        gx_full = sem("gx_full")
        gt_ready = sem("gt_ready")
        gl_full = sem("gl_full")
        gl_done = sem("gl_done")
        oh_ready = sem("onehot_ready")
        rank_full = sem("rank_full")
        route_ready = sem("route_ready")
        scattered = [sem(f"scattered{r}") for r in range(4)]
        gathered = [[sem(f"gathered{r}_{q}") for q in range(4)] for r in range(4)]
        xs_loaded = [sem(f"xs_loaded{s}") for s in range(2)]
        xt_full = sem("ffn_xt_full")
        xt_ready = sem("ffn_xt_ready")
        h_full = sem("ffn_h_full")
        h_added = sem("ffn_h_added")
        ht_full = sem("ffn_ht_full")
        ht_ready = sem("ffn_ht_ready")
        y_full = sem("ffn_y_full")
        y_ready = sem("ffn_y_ready")
        y_stored = [sem(f"y_stored{s}") for s in range(2)]
        an_ready = sem("an_ready")
        at_full = sem("at_full")
        at_ready = sem("at_ready")
        qk_full = sem("qk_full")
        qk_ready = sem("qk_ready")
        v_full = sem("v_full")
        v_ready = sem("v_ready")
        s_full = sem("scores_full")
        s_ready = sem("scores_ready")
        e_ready = sem("exp_ready")
        pt_ready = sem("probs_turned")
        pv_full = sem("pv_full")
        on_ready = sem("normalised_ready")
        ot_ready = sem("ot_ready")
        o_full = sem("o_full")
        o_read = sem("o_read")

        N_SMALL = 12
        block = ctx.enter_context(nc.Block())

        def done(J):
            return AHEAD + J + 1

        def slot_free(J):
            return AHEAD + J - 1

        def loads(I, s, i):
            return (I * ((FTILES + 1 - s) // 2) + i) * 16

        @block.sync
        def _(sp):
            sp.dma_start(C[:], consts).then_inc(w_small, 16)
            x_t = x.rearrange("b s d -> (b s) d").rearrange("(t p) d -> p t d", p=P)
            for h in range(2):
                sp.dma_start(X[:, h * HALF_TILES:(h + 1) * HALF_TILES, :],
                             x_t[:, h * HALF_TILES:(h + 1) * HALF_TILES, :]).then_inc(x_loaded[h], 16)
                if h == 0:
                    for dst, src in ((WQ, Wq), (WK, Wk), (WV, Wv), (WO, Wo)):
                        sp.dma_start(dst[:], src).then_inc(w_small, 16)
                    for c, b in enumerate((bq, bk, bv)):
                        sp.dma_start(BQKV[:, c:c + 1], b.rearrange("(p o) -> p o", o=1)).then_inc(w_small, 16)
                    sp.dma_start(BO[:], bo.partition_broadcast(P)).then_inc(w_small, 16)
                    sp.dma_start(GW[:], gate_w).then_inc(w_small, 16)
                    sp.dma_start(GB[:, 0, :], gate_b.partition_broadcast(P)).then_inc(w_small, 16)
                    sp.dma_start(GB[:, 1, :], expert_bias.partition_broadcast(P)).then_inc(w_small, 16)
            sp.wait_ge(zeros_ready, 1)
            for h in range(2):
                sp.dma_start(xs_d[h].rearrange("(j p) d -> p j d", p=P),
                             zeros[:].unsqueeze(1).broadcast_to([P, FTILES, D])).then_inc(pads_zeroed[h], 16)
            sp.dma_start(W1[:], w1.rearrange("e d f -> d e f")).then_inc(w_ffn, 16)
            sp.dma_start(B1[:], b1.partition_broadcast(P)).then_inc(w_ffn, 16)
            sp.dma_start(B2[:], b2.partition_broadcast(P)).then_inc(w_ffn, 16)
            sp.dma_start(W2[:], w2.rearrange("e (c p) n -> p e c n", p=P)).then_inc(w_ffn, 16)

            def load(I, j, s, i):
                sp.wait_ge(xt_full, slot_free(I * FTILES + j))
                sp.dma_start(xs[:, s, :], xs_d[I % 2][bass.ds(j * P, P), :]).then_inc(xs_loaded[s], 16)

            for I in range(4):
                sp.wait_ge(scattered[I], 16 * HALF_TILES)
                sp.wait_ge(xt_full, done(I * FTILES - 1))
                with sp.Fori(0, FTILES // 2) as i:
                    for s in range(2):
                        load(I, i * 2 + s, s, i)
                load(I, FTILES - 1, 0, FTILES // 2)

            o_t = out.rearrange("b s d -> (b s) d").rearrange("(t p) d -> p t d", p=P)
            for h in range(2):
                for q in range(4):
                    sp.wait_ge(dve_phase, 5 + 4 * h + q)
                    t = h * HALF_TILES + 4 * q
                    sp.dma_start(o_t[:, t:t + 4, :], X[:, t:t + 4, :]).then_inc(out_stored, 16)
            sp.wait_ge(out_stored, 16 * 8)

        @block.gpsimd
        def _(pool):
            pool.memset(zeros[:], 0.0).then_inc(zeros_ready, 1)
            pool.memset(VB[:], 0.0)
            pool.memset(KG[:], 0.0).then_inc(bufs_zeroed, 1)

            def spread(k, n):
                return range(HALF_TILES * k // n, HALF_TILES * (k + 1) // n)

            def scatter(I, tiles):
                pool.wait_ge(route_ready, I + 1)
                pool.wait_ge(gt_ready, AHEAD + PAIRS * (I + 1))
                pool.wait_ge(pads_zeroed[I % 2], 16)
                for t in tiles:
                    pool.indirect_dma_start(
                        out=xs_d[I % 2], out_offset=bass.IndirectOffsetOnAxis(ap=slot[I][:, t:t + 1], axis=0),
                        in_=XN[:, (I % 2) * HALF_TILES + t, :], in_offset=None).then_inc(scattered[I], 16)

            def gather(I, tiles):
                for s in range(2):
                    pool.wait_ge(y_stored[s], 16 + loads(I + 1, s, 0))
                for t in tiles:
                    pool.indirect_dma_start(
                        out=YG[:, (I % 2) * HALF_TILES + t, :], out_offset=None, in_=ys_d[I % 2],
                        in_offset=bass.IndirectOffsetOnAxis(ap=slot[I][:, t:t + 1], axis=0)
                    ).then_inc(gathered[I][t // 4], 16)

            chain = Chain(pool, pool_step)
            pool.memset(eps[:], EPS)
            chain.then(pool.memset(minus_half[:], -0.5))

            def rsqrt(n, norm):
                pool.wait_ge(mv_ready, norm + 1)
                chain.then(pool.tensor_tensor(var_eps[:, 0:n], mv[:, 0:n, 1], eps[:, 0:n], ALU.add))
                return pool.tensor_tensor(rstd[:, 0:n], var_eps[:, 0:n], minus_half[:, 0:n], ALU.pow)

            def normalised(dst, b, k):
                pool.sem_inc(pool_waits, 1)
                chain.then(pool.tensor_tensor(dst, x_of(b), mv[:, k:k + 2, 0:1].broadcast_to([P, 2, D]), ALU.subtract))
                return pool.tensor_tensor(dst, dst, rstd[:, k:k + 2].unsqueeze(2).broadcast_to([P, 2, D]), ALU.mult)

            def x_of(b):
                return X[:, bass.ds(b * 2, 2), :]

            def step(b, s, have):
                if have(3):
                    pool.tensor_tensor(x_of(b + 3), x_of(b + 3), YG[:, bass.ds((b + 3) * 2, 2), :],
                                       ALU.add).then_inc(x_mid, 1)
                if not have(3) and not have(-1):
                    return
                chain.then(rsqrt(4, b + (2 - FIRST_STEP)))
                if have(-1):
                    pool.wait_ge(gt_ready, AHEAD + TILES // 2 + b - 2)
                if have(3):
                    wait(pool, at_full, b + 2)
                if have(-1):
                    normalised(GN[:, 1 - s], b - 1, 2).then_inc(gn_ready, 1)
                if have(3):
                    normalised(AN[:, 1 - s], b + 3, 0).then_inc(an_ready, 1)
                    pool.wait_ge(an_ready, b + 4)
                    pool.sem_inc(pool_waits, 1)
                    pool.tensor_tensor(x_of(b + 3), x_of(b + 3), BO[:].unsqueeze(1).broadcast_to([P, 2, D]),
                                       ALU.add).then_inc(bo_added, 1)

            rsqrt(HALF_TILES, 0).then_inc(rstd_ready, 1)
            rsqrt(HALF_TILES, 1).then_inc(rstd_ready, 1)
            for I in range(2):
                scatter(I, range(HALF_TILES))
            gather(0, range(HALF_TILES))

            def before(b):
                if b == FIRST_STEP:
                    for q in range(4):
                        pool.wait_ge(gathered[0][q], 64)
                if b == LOOP[0]:
                    for q in range(4):
                        pool.wait_ge(gathered[1][q], 64)
                elif b < LOOP[0]:
                    gather(1, spread(b - FIRST_STEP, LOOP[0] - FIRST_STEP))
                else:
                    scatter(2, spread(b - LOOP[1], LAST_STEP - LOOP[1]))

            attention_schedule(pool, step, chain, STEPS_OF_POOL, before)
            scatter(3, range(HALF_TILES))
            gather(2, range(HALF_TILES))
            gather(3, range(HALF_TILES))

        @block.scalar
        def _(act):
            for c in (xt_ready, ht_ready, gt_ready):
                act.sem_inc(c, AHEAD)

            def gate_turned(G, s, tile):
                act.wait_ge(gn_ready, G + 1)
                nc.scalar.copy(XN[:, bass.ds(tile, 2), :], GN[:, s, :, :])
                act.wait_ge(gx_full, G + 1)
                act.wait_ge(gl_full, AHEAD + G)
                nc.scalar.copy(GT[:], PS[:, BANK_ACT, 0:2 * D]).then_inc(gt_ready, 1)

            def ffn(I):
                def xte(j, s):
                    J = I * FTILES + j
                    act.wait_ge(xt_full, done(J))
                    act.wait_ge(h_full, slot_free(J))
                    nc.scalar.copy(xT[:, s, :], PS[:, XT_B[s], 0:P]).then_inc(xt_ready, 1)

                def hte(j, s):
                    J = I * FTILES + j
                    act.wait_ge(ht_full, done(J))
                    act.wait_ge(y_full, slot_free(J))
                    nc.scalar.activation(hT[:, s].rearrange("p c t -> p (c t)"), PS[:, HT_B[s], :],
                                         ACT.Relu).then_inc(ht_ready, 1)

                def store(j, s):
                    act.wait_ge(y_ready, done(I * FTILES + j))
                    act.dma_start(ys_d[I % 2][bass.ds(j * P, P), :], ys[:, s, :]).then_inc(y_stored[s], 16)

                if I >= 2:
                    for q in range(4):
                        act.wait_ge(gathered[I - 2][q], 64)
                xte(0, 0)
                xte(1, 1)
                hte(0, 0)
                with act.Fori(0, (FTILES - 3) // 2) as i:
                    for k in range(2):
                        j = i * 2 + 1 + k
                        xte(j + 1, k)
                        hte(j, 1 - k)
                        store(j - 1, k)
                for j in (FTILES - 2, FTILES - 1):
                    if j + 1 < FTILES:
                        xte(j + 1, (j + 1) % 2)
                    hte(j, j % 2)
                    store(j - 1, (j - 1) % 2)
                store(FTILES - 1, (FTILES - 1) % 2)
                act.sem_inc(act_phase, 1)

            def at_copy(b, s):
                act.wait_ge(at_full, b + 1)
                wait(act, v_full, b - 1)
                nc.scalar.copy(AT[:, s, :], PS[:, BANK_ACT, 0:SEQ]).then_inc(at_ready, 1)

            def qk_copy(b, s):
                act.wait_ge(qk_full, b + 1)
                wait(act, s_full, 2 * b - 2)
                for h in range(4):
                    nc.scalar.activation(QH[:, s, h, :], PS[:, BANK_ACT, 0:SEQ], ACT.Identity,
                                         bias=BQM[:, h:h + 1], scale=const("head_col")[:, h:h + 1])
                for g in range(G4):
                    r = slice(32 * g, 32 * g + 32)
                    last = nc.scalar.activation(KG[r, s, g, QB:KPAD], PS[r, BANK_ACT, SEQ:2 * SEQ], ACT.Identity,
                                                bias=BQKV[r, 1:2])
                last.then_inc(qk_ready, 1)

            def exp(b, u):
                act.wait_ge(s_ready, 2 * b + u + 1)
                nc.scalar.activation(E[:, u, :], E[:, u, :], ACT.Exp, scale=SCALE).then_inc(e_ready, 1)

            def ot_bias(b):
                act.wait_ge(on_ready, b + 1)
                wait(act, o_full, b)
                nc.scalar.activation(OT[:], ON[:], ACT.Identity, bias=BQKV[:, 2:3]).then_inc(ot_ready, 1)

            def values(b, s):
                act.wait_ge(v_full, b + 1)
                wait(act, pv_full, b - 1)
                for r in range(4):
                    rows = slice(32 * r, 32 * r + 32)
                    last = nc.scalar.copy(
                        VB[rows, s].rearrange("p k (g r j) -> p (k g) r j", r=4, j=HD)[:, :, r, :],
                        PS[rows, BANK_ACT, 2 * D:].rearrange("p (m j) -> p m j", j=HD))
                last.then_inc(v_ready, 1)

            def step(b, s, have):
                if have(0):
                    exp(b, 0)
                if have(-2):
                    gate_turned(TILES // 2 + b - 2, s, (b - 2) * 2)
                if have(1):
                    values(b + 1, 1 - s)
                if have(0):
                    exp(b, 1)
                if have(2):
                    at_copy(b + 2, s)
                if have(-1):
                    ot_bias(b - 1)
                if have(2):
                    qk_copy(b + 2, s)

            act.wait_ge(const_ready, 1)
            act.wait_ge(bufs_zeroed, 1)
            for h in range(2):
                with act.Fori(0, PAIRS // 2) as i:
                    for s in range(2):
                        gate_turned(i * 2 + h * PAIRS + s, s, i * 4 + h * HALF_TILES + 2 * s)
            act.wait_ge(w_ffn, 64)
            nc.scalar.mul(B2[:], B2[:], 0.5)
            nc.scalar.mul(W2[:], W2[:], 0.5).then_inc(w2_halved, 1)
            act.sem_inc(act_phase, 1)
            ffn(0)
            ffn(1)
            attention_schedule(act, step)
            act.sem_inc(act_phase, 1)
            ffn(2)
            ffn(3)

        @block.vector
        def _(dve):
            chain = Chain(dve, dve_step)
            e = Experts(dve, "dve")
            for c in (h_added, y_ready, gl_done):
                dve.sem_inc(c, AHEAD)
            for s in range(2):
                dve.sem_inc(y_stored[s], 16)
            dve.wait_ge(w_small, 16 * N_SMALL)
            nc.vector.tensor_copy(ident_b[:], ident)
            nc.vector.tensor_copy(mask_b[:], const("mask"))
            nc.vector.tensor_copy(mask_first_b[:], const("mask_first"))
            nc.vector.tensor_copy(before_b[:], const("before"))
            nc.vector.tensor_copy(ones_b[:], const("ones"))
            nc.vector.tensor_scalar(BQM[:], const("head_col"), BQKV[:, 0:1], None, ALU.mult).then_inc(const_ready, 1)

            def statistics(k, n):
                dve.sem_inc(norm_waits, 1)
                for t in range(k, k + n):
                    last = nc.vector.bn_aggr(mv[:, t, :], stats[:, t, :])
                return last

            def tile_statistics(tile, k):
                return nc.vector.bn_stats(stats[:, bass.ds(k, 1), :].rearrange("p o c -> p (o c)"), x_tile(tile))

            def normalised(dst, tile, k):
                m = mv[:, bass.ds(k, 1), 0:1].rearrange("p o c -> p (o c)")
                return nc.vector.tensor_scalar(dst, x_tile(tile), m, rstd[:, bass.ds(k, 1)],
                                               ALU.subtract, ALU.mult)

            def x_tile(tile):
                return X[:, bass.ds(tile, 1), :].rearrange("p o d -> p (o d)")

            def half_statistics(h):
                dve.sem_inc(norm_waits, 1)
                with dve.Fori(0, HALF_TILES // 4) as i:
                    chain.enter(i, 1)
                    for t in range(4):
                        last = tile_statistics(i * 4 + (h * HALF_TILES + t), i * 4 + t)
                    chain.k += 1
                    last.then_inc(dve_step, 1)
                    chain.leave(HALF_TILES // 4)
                dve.wait_ge(dve_step, chain.base)
                statistics(0, HALF_TILES).then_inc(mv_ready, 1)
                dve.wait_ge(rstd_ready, h + 1)

            def gate_norm(G, s, tile, k):
                dve.wait_ge(gt_ready, AHEAD + G - 1)
                for t in range(2):
                    last = normalised(GN[:, s, t, :], tile + t, k + t)
                last.then_inc(gn_ready, 1)

            def gate_logits(G, tile):
                dve.wait_ge(gl_full, AHEAD + G + 1)
                chain.then(nc.vector.tensor_tensor(
                    L0[:], PS[:, BANK_DVE, 2 * D:2 * D + 2 * EXPERTS].rearrange("p (t e) -> p t e", t=2),
                    GB[:, 0, :].unsqueeze(1).broadcast_to([P, 2, EXPERTS]), ALU.add))
                nc.vector.tensor_tensor(L[:, bass.ds(tile, 2), :], L0[:],
                                        GB[:, 1, :].unsqueeze(1).broadcast_to([P, 2, EXPERTS]),
                                        ALU.add).then_inc(gl_done, 1)

            def route(I):
                shape = [P, HALF_TILES, EXPERTS]
                logits = L[:, (I % 2) * HALF_TILES:(I % 2 + 1) * HALF_TILES, :]
                dve.wait_ge(gl_done, AHEAD + PAIRS * (I + 1))
                chain.then(nc.vector.tensor_reduce(r_max[:], logits, AX.X, ALU.max))
                chain.then(nc.vector.tensor_tensor(r_a[:], logits, r_max[:].unsqueeze(2).broadcast_to(shape),
                                                   ALU.is_ge))
                chain.then(nc.vector.tensor_tensor(r_b[:], r_a[:], const("rank_down").unsqueeze(1).broadcast_to(shape),
                                                   ALU.mult))
                chain.then(nc.vector.tensor_reduce(r_max[:], r_b[:], AX.X, ALU.max))
                nc.vector.tensor_tensor(onehot[:], r_b[:], r_max[:].unsqueeze(2).broadcast_to(shape),
                                        ALU.is_equal).then_inc(oh_ready, 1)
                dve.wait_ge(rank_full, I + 1)
                chain.then(nc.vector.tensor_copy(r_cnt[:], PS[:, BANK_DVE, P:P + EXPERTS]))
                chain.then(nc.vector.tensor_tensor(
                    r_steps[:], r_cnt[:].unsqueeze(2).broadcast_to([P, EXPERTS, HALF_TILES]),
                    const("tile_steps").unsqueeze(1).broadcast_to([P, EXPERTS, HALF_TILES]), ALU.is_gt))
                chain.then(nc.vector.tensor_reduce(r_tiles[:], r_steps[:], AX.X, ALU.add))
                chain.then(nc.vector.tensor_tensor(
                    r_pre[:], r_tiles[:].unsqueeze(1).broadcast_to([P, EXPERTS, EXPERTS]),
                    const("earlier_expert").rearrange("p (e f) -> p e f", e=EXPERTS), ALU.mult))
                chain.then(nc.vector.tensor_reduce(r_first[:], r_pre[:], AX.X, ALU.add))
                chain.then(nc.vector.tensor_tensor(r_end[:], r_first[:], r_tiles[:], ALU.add))
                chain.then(nc.vector.scalar_tensor_tensor(
                    out=r_a[:], in0=r_first[:].unsqueeze(1).broadcast_to(shape), scalar=float(P),
                    in1=PS[:, BANK_DVE, 0:P].rearrange("p (t e) -> p t e", e=EXPERTS), op0=ALU.mult, op1=ALU.add))
                chain.then(nc.vector.tensor_tensor(r_b[:], r_a[:], onehot[:], ALU.mult))
                chain.then(nc.vector.tensor_reduce(r_slot[:], r_b[:], AX.X, ALU.add))
                nc.vector.tensor_copy(slot[I][:], r_slot[:])
                chain.then(nc.vector.tensor_tensor(
                    r_ge[:], const("tile_number").rearrange("p (j e) -> p j e", e=EXPERTS),
                    r_end[:].unsqueeze(1).broadcast_to([P, EWORDS * EDIGITS, EXPERTS]), ALU.is_ge))
                chain.then(nc.vector.tensor_reduce(r_et[:], r_ge[:], AX.X, ALU.add))
                chain.then(nc.vector.tensor_scalar(r_et[:], r_et[:], float(EXPERTS - 1), None, ALU.min))
                chain.then(nc.vector.tensor_tensor(
                    r_digits[:], r_et[:].rearrange("p (w k) -> p w k", k=EDIGITS),
                    const("digit").unsqueeze(1).broadcast_to([P, EWORDS, EDIGITS]), ALU.mult))
                chain.then(nc.vector.tensor_reduce(r_words[:], r_digits[:], AX.X, ALU.add))
                nc.vector.tensor_copy(experts_of[I][:], r_words[:]).then_inc(route_ready, 1)

            def ffn(I):
                def add_b1(j, s, expert):
                    J = I * FTILES + j
                    dve.wait_ge(h_full, done(J))
                    dve.wait_ge(ht_full, slot_free(J))
                    nc.vector.tensor_tensor(hp[:, s, :], PS[:, H_B[s], :],
                                            B1[:, bass.ds(expert, 1), :].rearrange("p o f -> p (o f)"),
                                            ALU.add).then_inc(h_added, 1)

                def add_b2(j, s, i, expert):
                    J = I * FTILES + j
                    dve.wait_ge(y_full, done(J))
                    dve.wait_ge(y_stored[s], 16 + loads(I, s, i))
                    nc.vector.tensor_tensor(ys[:, s, :], PS[:, Y_B[s], 0:D],
                                            B2[:, bass.ds(expert, 1), :].rearrange("p o f -> p (o f)"),
                                            ALU.add).then_inc(y_ready, 1)

                e.load(experts_of[I])
                add_b1(0, 0, e.next(0))
                add_b1(1, 1, e.next(1))
                with dve.Fori(0, FPAIRS - 1) as i:
                    for s in range(2):
                        add_b2(i * 2 + s, s, i, e.next(s))
                        add_b1(i * 2 + s + 2, s, e.next(s + 2))
                    e.passed(2)
                j = FTILES - 3
                add_b2(j, 0, FPAIRS - 1, e.next(0))
                add_b1(j + 2, 0, e.next(2))
                add_b2(j + 1, 1, FPAIRS - 1, e.next(1))
                add_b2(j + 2, 0, FPAIRS, e.next(2))

            def add_ffn(tile, n):
                xt = X[:, tile:tile + n, :]
                return nc.vector.tensor_tensor(xt, xt, YG[:, tile:tile + n, :], ALU.add)

            def softmax(b, u):
                sc = PS[:, 2 * u:2 * u + 2, :].rearrange("p k (m n) -> p (k m) n", n=2 * QB)
                dve.wait_ge(s_full, 2 * b + u + 1)
                chain.then(nc.vector.tensor_reduce(top[:, u, :], sc, AX.X, ALU.max))
                nc.vector.tensor_tensor(E[:, u, :].rearrange("p (m n) -> p m n", n=2 * QB), sc,
                                        top[:, u, :].unsqueeze(2).broadcast_to([P, 16, 2 * QB]),
                                        ALU.subtract).then_inc(s_ready, 1)

            def turn(b, s, u):
                dve.wait_ge(e_ready, 2 * b + u + 1)
                wait(dve, pv_full, b - 1)
                at = 4 * u * 256 + QB
                dst = PT[:, s, :]
                dst = bass.AP(dst.tensor, dst.offset + at, [dst.ap[0], [2 * QB, 16], [256 - QB, 2], [1, QB]])
                nc.vector.transpose(dst, E[:, u, :].rearrange("p (m k n) -> p m k n", k=2, n=QB)).then_inc(pt_ready, 1)

            def normalise(b, s):
                dve.wait_ge(pv_full, b + 1)
                chain.then(nc.vector.reciprocal(rden[:], PS[:, ND[s], SEQ:2 * SEQ]))
                wait(dve, ot_ready, b)
                nc.vector.tensor_tensor(ON[:], PS[:, ND[s], 0:SEQ], rden[:], ALU.mult).then_inc(on_ready, 1)

            def residual(b):
                dve.wait_ge(o_full, b + 1)
                dve.wait_ge(bo_added, b + 1)
                xt = X[:, bass.ds(b * 2, 2), :]
                nc.vector.tensor_tensor(xt, xt, PS[:, BANK_DVE, 0:2 * D].rearrange("p (t n) -> p t n", t=2),
                                        ALU.add).then_inc(o_read, 1)

            def step(b, s, have):
                if have(-1):
                    turn(b - 1, 1 - s, 1)
                if have(0):
                    softmax(b, 0)
                    softmax(b, 1)
                if have(-1):
                    normalise(b - 1, 1 - s)
                if have(0):
                    turn(b, s, 0)
                if have(3):
                    dve.wait_ge(x_mid, b + 4)
                    dve.sem_inc(norm_waits, 1)
                    for t in range(2):
                        last = tile_statistics((b + 3) * 2 + t, t)
                if have(-2):
                    dve.wait_ge(gl_full, AHEAD + TILES // 2 + b - 1)
                if have(-1):
                    residual(b - 1)
                if have(-2):
                    gate_logits(TILES // 2 + b - 2, (b - 2) * 2)
                if have(-1):
                    dve.wait_ge(o_read, b)
                    dve.sem_inc(norm_waits, 1)
                    for t in range(2):
                        last = tile_statistics((b - 1) * 2 + t, 2 + t)
                if have(3) or have(-1):
                    chain.then(last)
                    wait(dve, an_ready, b + 3 if have(3) else BATCH)
                    if have(-2):
                        dve.wait_ge(gn_ready, TILES // 2 + b - 1)
                    first, end = 0 if have(3) else 2, 4 if have(-1) else 2
                    statistics(first, end - first).then_inc(mv_ready, 1)

            for h in range(2):
                dve.wait_ge(x_loaded[h], 16)
                t0 = h * HALF_TILES
                half_statistics(h)
                gate_norm(h * PAIRS, 0, t0, 0)
                with dve.Fori(0, PAIRS // 2 - 1) as i:
                    chain.enter(i, 2)
                    for k in range(2):
                        pair = i * 2 + k
                        gate_norm(pair + (h * PAIRS + 1), 1 - k, pair * 2 + (t0 + 2), pair * 2 + 2)
                        gate_logits(pair + h * PAIRS, pair * 2 + t0)
                    chain.leave(PAIRS // 2 - 1)
                gate_norm((h + 1) * PAIRS - 1, 1, t0 + HALF_TILES - 2, HALF_TILES - 2)
                for pair in (PAIRS - 2, PAIRS - 1):
                    gate_logits(h * PAIRS + pair, pair * 2 + t0)
                route(h)
            dve.sem_inc(dve_phase, 1)
            dve.wait_ge(w_ffn, 64)
            dve.wait_ge(w2_halved, 1)
            ffn(0)
            ffn(1)
            dve.sem_inc(dve_phase, 1)

            def after_loop():
                route(2)
                dve.sem_inc(dve_phase, 1)

            attention_schedule(dve, step, chain, STEPS_OF_DVE, after_loop=after_loop)
            route(3)
            dve.sem_inc(dve_phase, 1)
            ffn(2)
            ffn(3)
            for h in range(2):
                for q in range(4):
                    dve.wait_ge(gathered[2 + h][q], 64)
                    add_ffn(h * HALF_TILES + 4 * q, 4).then_inc(dve_phase, 1)

        @block.tensor
        def _(pe):
            e = Experts(pe, "pe")
            for c in (xt_full, h_full, ht_full, y_full, gl_full):
                pe.sem_inc(c, AHEAD)

            def mm(*a, **k):
                return nc.tensor.matmul(*a, skip_group_check=True, **k)

            def gate_turn(G, s):
                pe.wait_ge(gn_ready, G + 1)
                pe.wait_ge(gt_ready, AHEAD + G)
                for t in range(2):
                    last = nc.tensor.transpose(PS[:, BANK_ACT, t * P:(t + 1) * P], GN[:, s, t, :], ident)
                last.then_inc(gx_full, 1)

            def gate_mm(G):
                pe.wait_ge(gt_ready, AHEAD + G + 1)
                pe.wait_ge(gl_done, AHEAD + G)
                for t in range(2):
                    last = mm(PS[:, BANK_DVE, 2 * D + t * EXPERTS:2 * D + (t + 1) * EXPERTS], GT[:, t * P:(t + 1) * P], GW[:],
                              start=True, stop=True)
                last.then_inc(gl_full, 1)

            def route(I):
                pe.wait_ge(oh_ready, I + 1)
                pe.wait_ge(gl_done, AHEAD + PAIRS * (I + 1))
                oh = onehot[:].rearrange("p t e -> p (t e)")
                mm(PS[:, BANK_DVE, 0:P], before_b[:], oh, start=True, stop=False)
                for k in range(1, HALF_TILES):
                    mm(PS[:, BANK_DVE, k * EXPERTS:P], ones_b[:], oh[:, 0:P - k * EXPERTS], start=False, stop=False)
                for k in range(HALF_TILES):
                    last = mm(PS[:, BANK_DVE, P:P + EXPERTS], ones_b[:], oh[:, k * EXPERTS:(k + 1) * EXPERTS],
                              start=False, stop=(k == HALF_TILES - 1))
                last.then_inc(rank_full, 1)

            def ffn(I):
                def turn_x(j, s, i):
                    J = I * FTILES + j
                    pe.wait_ge(xs_loaded[s], 16 + loads(I, s, i))
                    pe.wait_ge(xt_ready, slot_free(J))
                    nc.tensor.transpose(PS[:, XT_B[s], 0:P], xs[:, s, :], ident).then_inc(xt_full, 1)

                def up(j, s, expert):
                    J = I * FTILES + j
                    pe.wait_ge(xt_ready, done(J))
                    pe.wait_ge(h_added, slot_free(J))
                    mm(PS[:, H_B[s], :], xT[:, s, :], W1[:, bass.ds(expert, 1), :].rearrange("p o f -> p (o f)"),
                       start=True, stop=True).then_inc(h_full, 1)

                def turn_h(j, s):
                    J = I * FTILES + j
                    pe.wait_ge(h_added, done(J))
                    pe.wait_ge(ht_ready, slot_free(J))
                    for c in range(FC):
                        last = nc.tensor.transpose(PS[:, HT_B[s], c * P:(c + 1) * P], hp[:, s, c * P:(c + 1) * P],
                                                   ident)
                    last.then_inc(ht_full, 1)

                def down(j, s, expert):
                    J = I * FTILES + j
                    pe.wait_ge(ht_ready, done(J))
                    pe.wait_ge(y_ready, slot_free(J))
                    for c in range(FC):
                        last = mm(PS[:, Y_B[s], 0:D], hT[:, s, c, :],
                                  W2[:, bass.ds(expert, 1), c, :].rearrange("p o n -> p (o n)"),
                                  start=(c == 0), stop=(c == FC - 1))
                    last.then_inc(y_full, 1)

                pe.wait_ge(w2_halved, 1)
                pe.wait_ge(route_ready, I + 1)
                turn_x(0, 0, 0)
                e.load(experts_of[I])
                up(0, 0, e.next(0))
                turn_x(1, 1, 0)
                turn_h(0, 0)
                up(1, 1, e.next(1))
                with pe.Fori(0, FPAIRS - 1) as i:
                    for s in range(2):
                        j = i * 2 + s
                        turn_x(j + 2, s, i + 1)
                        down(j, s, e.next(s))
                        turn_h(j + 1, 1 - s)
                        up(j + 2, s, e.next(s + 2))
                    e.passed(2)
                j = FTILES - 3
                turn_x(j + 2, 0, FPAIRS)
                down(j, 0, e.next(0))
                turn_h(j + 1, 1)
                up(j + 2, 0, e.next(2))
                down(j + 1, 1, e.next(1))
                turn_h(j + 2, 0)
                down(j + 2, 0, e.next(2))

            def turn_a(b, s):
                pe.wait_ge(an_ready, b + 1)
                for t in range(2):
                    last = nc.tensor.transpose(PS[:, BANK_ACT, t * P:(t + 1) * P], AN[:, s, t, :], ident)
                last.then_inc(at_full, 1)

            def project_qk(b, s):
                pe.wait_ge(at_ready, b + 1)
                mm(PS[:, BANK_ACT, 0:SEQ], WQ[:], AT[:, s, :], start=True, stop=True)
                mm(PS[:, BANK_ACT, SEQ:2 * SEQ], WK[:], AT[:, s, :], start=True, stop=True).then_inc(qk_full, 1)

            def project_v(b, s):
                pe.wait_ge(at_ready, b + 1)
                for k in range(NQB):
                    for r in range(4):
                        last = mm(PS[32 * r:32 * r + 32, BANK_ACT, 2 * D + k * 32:2 * D + (k + 1) * 32],
                                  AT[:, s, k * QB:(k + 1) * QB],
                                  WV[:].rearrange("p (g r j) -> p g r j", r=4, j=HD)[:, :, r, :],
                                  start=True, stop=True)
                last.then_inc(v_full, 1)

            def scores(b, s, u):
                pe.wait_ge(qk_ready, b + 1)
                wait(pe, s_ready, 2 * b + u - 1)
                for k in range(2):
                    mask = mask_first_b if u == 0 and k == 0 else mask_b
                    mm(PS[:, 2 * u + k, :], ident_b[:], mask[:], start=True, stop=False)
                    for c in range(2):
                        q = QB * (4 * u + 2 * k + c)
                        for h in range(4):
                            last = mm(PS[32 * h:32 * h + 32, 2 * u + k, 256 * c:256 * c + 256],
                                      QH[:, s, h, q:q + QB], KG[:, s, :, q:q + 2 * QB], start=False, stop=True)
                last.then_inc(s_full, 1)

            def weigh(b, s, u):
                pe.wait_ge(pt_ready, 2 * b + u + 1)
                pe.wait_ge(v_ready, b + 1)
                if u == 0:
                    wait(pe, on_ready, b - 1)
                for kb in (range(3) if u == 0 else range(3, NQB)):
                    n = min(2 * QB, SEQ - kb * QB)
                    for g in range(G4):
                        rhs = PT[:, s, (kb + 1) * 256 + g * 64:(kb + 1) * 256 + g * 64 + n]
                        r = slice(32 * g, 32 * g + 32)
                        mm(PS[r, ND[s], kb * QB:kb * QB + n], VB[:, s, kb, r], rhs, start=(kb == 0), stop=False)
                        last = mm(PS[r, ND[s], SEQ + kb * QB:SEQ + kb * QB + n], bd_ones(g), rhs, start=False,
                                  stop=True)
                if u == 1:
                    last.then_inc(pv_full, 1)

            def bd_ones(g):
                return const("head_row_bd")[:, 32 * g:32 * g + 32]

            def project_o(b):
                pe.wait_ge(ot_ready, b + 1)
                for t in range(2):
                    last = mm(PS[:, BANK_DVE, t * D:(t + 1) * D], OT[:, t * P:(t + 1) * P], WO[:],
                              start=True, stop=True)
                last.then_inc(o_full, 1)

            def step(b, s, have):
                if have(-1):
                    weigh(b - 1, 1 - s, 1)
                if have(1) or have(-2):
                    wait(pe, qk_ready, b + 2 if have(1) else BATCH)
                if have(1):
                    project_v(b + 1, 1 - s)
                if have(-2):
                    gate_turn(TILES // 2 + b - 2, s)
                if have(1):
                    scores(b + 1, 1 - s, 0)
                if have(2):
                    if have(-2):
                        pe.wait_ge(gt_ready, AHEAD + TILES // 2 + b - 1)
                    if have(1):
                        pe.wait_ge(v_ready, b + 2)
                    turn_a(b + 2, s)
                if have(1):
                    scores(b + 1, 1 - s, 1)
                if have(-1):
                    wait(pe, o_read, b - 1)
                    wait(pe, gl_done, AHEAD + TILES // 2 + b - 2)
                    project_o(b - 1)
                if have(-2):
                    gate_mm(TILES // 2 + b - 2)
                if have(2):
                    project_qk(b + 2, s)
                if have(0):
                    weigh(b, s, 0)

            pe.wait_ge(w_small, 16 * N_SMALL)
            pe.wait_ge(const_ready, 1)
            for h in range(2):
                with pe.Fori(0, PAIRS // 2) as i:
                    for s in range(2):
                        gate_turn(i * 2 + h * PAIRS + s, s)
                        gate_mm(i * 2 + h * PAIRS + s)
                route(h)
            pe.wait_ge(w_ffn, 64)
            pe.wait_ge(act_phase, 1)
            pe.wait_ge(dve_phase, 1)
            ffn(0)
            ffn(1)
            pe.wait_ge(act_phase, 3)
            pe.wait_ge(dve_phase, 2)

            def after_loop():
                route(2)
                pe.wait_ge(dve_phase, 3)

            attention_schedule(pe, step, after_loop=after_loop)
            pe.wait_ge(gl_done, AHEAD + TILES)
            route(3)
            pe.wait_ge(act_phase, 4)
            pe.wait_ge(dve_phase, 4)
            ffn(2)
            ffn(3)


def attention_schedule(eng, step, chain=None, steps=0, before=lambda b: None, after_loop=lambda: None):
    def straight(b):
        before(b)
        step(b, b % 2, lambda k: 0 <= b + k < BATCH)

    for b in range(FIRST_STEP, LOOP[0]):
        straight(b)
    before(LOOP[0])
    count = (LOOP[1] - LOOP[0]) // 2
    with eng.Fori(0, count) as i:
        if chain:
            chain.enter(i, 2 * steps)
        for s in range(2):
            step(i * 2 + (LOOP[0] + s), s, lambda k: True)
        if chain:
            chain.leave(count)
    after_loop()
    for b in range(LOOP[1], LAST_STEP):
        straight(b)


FIRST_STEP, LAST_STEP = -3, BATCH + 2
LOOP = (2, BATCH - 4)
STEPS_OF_DVE = 5
STEPS_OF_POOL = 4


_INS = ["L0_attn_x", "L0_attn_Wq", "L0_attn_bq", "L0_attn_Wk", "L0_attn_bk", "L0_attn_Wv", "L0_attn_bv",
        "L0_attn_Wo", "L0_attn_bo", "L0_ffn_gate_w", "L0_ffn_gate_b", "L0_ffn_expert_bias", "L0_ffn_w1",
        "L0_ffn_b1", "L0_ffn_w2", "L0_ffn_b2"]


def kernel(**inputs):
    import concourse.bacc as bacc
    from concourse.bass_utils import run_bass_kernel_spmd

    nc = bacc.Bacc("TRN2", target_bir_lowering=False, num_devices=1)
    arrays, args = {}, []
    for name, a in [(n, inputs[n]) for n in _INS] + [("constants", constants())]:
        a = np.ascontiguousarray(np.asarray(a).T if name == "L0_ffn_gate_w" else a)
        arrays[f"in_{name}"] = a
        args.append(nc.dram_tensor(f"in_{name}", a.shape, mybir.dt.from_np(a.dtype), kind="ExternalInput").ap())
    args.append(nc.dram_tensor("out_x", (BATCH, SEQ, D), F32, kind="ExternalOutput").ap())
    macaron(nc, *args)
    r = run_bass_kernel_spmd(nc, [arrays], core_ids=[0])
    return r.results[0]["out_x"]
```

```python
from contextlib import ExitStack

import numpy as np

import concourse.bass as bass
from concourse import mybir

F32 = mybir.dt.float32
BF16 = mybir.dt.bfloat16
I32 = mybir.dt.int32
ALU = mybir.AluOpType
ACT = mybir.ActivationFunctionType
AX = mybir.AxisListType

P = 128
BATCH, SEQ, D = 16, 256, 128
HEADS, HD, WINDOW = 16, 8, 32
EXPERTS, DFF = 8, 512
EPS = 1e-5
NEG = -1e30
TOKENS = BATCH * SEQ
TILES = TOKENS // P
HALF_TILES = TILES // 2
HALF_TOKENS = TOKENS // 2
GROUP = 4
GATES0 = TILES // GROUP


def gates(I):
    return (I + 1) * GATES0 // 2 if I < 2 else GATES0 + (I - 1) * BATCH // 2


FTILES = (HALF_TOKENS + EXPERTS * (P - 1)) // P
FLOOPS, FREST = divmod(FTILES, 4)
assert FREST == 3
EBITS = 3
EDIGITS = 24 // EBITS
EWORDS = -(-FTILES // EDIGITS)
FC = DFF // P
QB = 32
NQB = SEQ // QB
G4 = HEADS // 4
KPAD = QB + SEQ
SCALE = float(HD) ** -0.5
AHEAD = 4

CONSTS = {}
_at = 0
for _name, _n in (("ident", P), ("mask", 2 * QB), ("mask_first", 2 * QB), ("head_col", 4), ("head_row_bd", P),
                  ("before", P), ("rank_down", EXPERTS), ("tile_steps", HALF_TILES),
                  ("earlier_expert", EXPERTS * EXPERTS), ("tile_number", EWORDS * EDIGITS), ("digit", EDIGITS)):
    CONSTS[_name] = (_at, _n)
    _at += _n
N_CONSTS = _at


def constants():
    c = np.zeros((P, N_CONSTS), np.float32)

    def put(name, a):
        at, n = CONSTS[name]
        c[:, at:at + n] = np.broadcast_to(a, (P, n))

    p = np.arange(P)
    q, k = (p % QB)[:, None], np.arange(2 * QB)[None, :]
    allowed = np.where(k < QB, k > q, k - QB <= q)
    block = np.where(allowed, 0.0, NEG)
    no_previous = np.where(allowed & (k >= QB), 0.0, NEG)
    put("ident", np.eye(P))
    put("mask", block)
    put("mask_first", no_previous)
    put("head_col", (p[:, None] // HD) % 4 == np.arange(4)[None, :])
    put("head_row_bd", (p[None, :] // HD) % 4 == p[:, None] // QB)
    put("before", p[:, None] < p[None, :])
    e = np.arange(EXPERTS)
    put("rank_down", (EXPERTS - e)[None, :])
    put("tile_steps", (P * np.arange(HALF_TILES))[None, :])
    put("earlier_expert", (e[None, :] < e[:, None]).reshape(1, -1))
    put("tile_number", np.arange(EWORDS * EDIGITS)[None, :])
    put("digit", (float(EXPERTS) ** np.arange(EDIGITS))[None, :])
    return c


ID_RUN = 4


def numbers():
    tile, p = np.arange(HALF_TILES + FTILES), np.arange(P)
    return np.repeat((tile[None, :] * P + p[:, None]).astype(np.int32), ID_RUN, axis=1)


def wait(eng, sem, value):
    if isinstance(value, int) and value <= 0:
        return
    eng.wait_ge(sem, value)


class Experts:

    def __init__(self, eng, name):
        self.eng = eng
        self.words = [eng.alloc_register(f"{name}_experts{w}") for w in range(EWORDS)]
        self.moved = eng.alloc_register(f"{name}_moved")
        self.spare = eng.alloc_register(f"{name}_spare")

    def load(self, table):
        for w, word in enumerate(self.words):
            self.eng.reg_load(word, table[0:1, w:w + 1])

    def next(self, k):
        e = (self.eng.snap(self.words[0]) // EXPERTS ** k) % EXPERTS
        return self.eng.snap(e, min_val=0, max_val=EXPERTS - 1)

    def move(self, n):
        bits = EBITS * n
        top = self.words[1:]
        self.take(self.moved, top[0], bits)
        for word, above in zip(top, top[1:] + [None]):
            self.eng.reg_alu(word, word, bits, ALU.logical_shift_right)
            if above is not None:
                self.take(self.spare, above, bits)
                self.eng.reg_alu(word, word, self.spare, ALU.add)

    def take(self, out, word, bits):
        self.eng.reg_alu(out, word, (1 << bits) - 1, ALU.bitwise_and)
        self.eng.reg_alu(out, out, EBITS * EDIGITS - bits, ALU.logical_shift_left)

    def passed(self, n):
        self.eng.reg_alu(self.words[0], self.words[0], EBITS * n, ALU.logical_shift_right)
        self.eng.reg_alu(self.words[0], self.words[0], self.moved, ALU.add)


class Chain:

    def __init__(self, eng, sem):
        self.eng, self.sem, self.base, self.k = eng, sem, 0, 0

    def then(self, ins):
        self.k += 1
        ins.then_inc(self.sem, 1)
        self.eng.wait_ge(self.sem, self.base + self.k)

    def enter(self, i, per):
        self.start, self.base, self.k, self.per = self.base + self.k, self.base + self.k + i * per, 0, per

    def leave(self, count):
        assert self.k == self.per, f"{self.k} steps in a loop's body"
        self.base, self.k = self.start + count * self.per, 0


def macaron(nc, x, Wq, bq, Wk, bk, Wv, bv, Wo, bo, gate_w, gate_b, expert_bias, w1, b1, w2, b2, consts, ids, out):
    with ExitStack() as ctx:
        def sb(name, shape, dt=F32):
            return ctx.enter_context(nc.sbuf_tensor(name, shape, dt))

        def sem(name):
            return ctx.enter_context(nc.semaphore(name))

        X = sb("X", [P, TILES, D])
        XN = sb("XN", [P, TILES, D])
        YG = sb("YG", [P, TILES, D])
        W1 = sb("W1", [P, EXPERTS, DFF])
        W2 = sb("W2", [P, EXPERTS, FC, D])
        B1 = sb("B1", [P, EXPERTS, FC])
        B2 = sb("B2", [P, EXPERTS, D])
        WQ, WK, WV, WO = (sb(n, [P, D]) for n in ("WQ", "WK", "WV", "WO"))
        BQKV = sb("BQKV", [P, 3])
        BO = sb("BO", [P, D])
        GW = sb("GW", [P, EXPERTS])
        GB = sb("GB", [P, 2, EXPERTS])
        C = sb("C", [P, N_CONSTS])

        def const(name):
            at, n = CONSTS[name]
            return C[:, at:at + n]

        ident = const("ident")
        ident_b = sb("ident_b", [P, P], BF16)
        mask_b = sb("mask_b", [P, 512], BF16)
        mask_first_b = sb("mask_first_b", [P, 512], BF16)
        before_b = sb("before_b", [P, P], BF16)
        ones_b = sb("ones_b", [P, P], BF16)
        BQM = sb("BQM", [P, 4])

        GN = sb("GN", [P, 2, GROUP, D])
        GT = sb("GT", [P, 2, GROUP * D])
        L = sb("L", [P, TILES, EXPERTS])
        L0 = sb("L0", [P, GROUP, EXPERTS])
        stats = sb("stats", [P, TILES, 6])
        mv = sb("mv", [P, TILES, 2])
        var_eps = sb("var_eps", [P, TILES])
        rstd = sb("rstd", [P, TILES])
        eps = sb("eps", [P, TILES])
        minus_half = sb("minus_half", [P, TILES])
        r_max = sb("r_max", [P, HALF_TILES])
        r_a = sb("r_a", [P, HALF_TILES, EXPERTS])
        r_b = sb("r_b", [P, HALF_TILES, EXPERTS])
        onehot = sb("onehot", [P, HALF_TILES, EXPERTS], BF16)
        r_cnt = sb("r_cnt", [P, EXPERTS])
        r_steps = sb("r_steps", [P, EXPERTS, HALF_TILES])
        r_tiles = sb("r_tiles", [P, EXPERTS])
        r_pre = sb("r_pre", [P, EXPERTS, EXPERTS])
        r_first = sb("r_first", [P, EXPERTS])
        r_end = sb("r_end", [P, EXPERTS])
        r_ge = sb("r_ge", [P, EWORDS * EDIGITS, EXPERTS])
        r_et = sb("r_et", [P, EWORDS * EDIGITS])
        r_slot = sb("r_slot", [P, HALF_TILES])
        slot = [sb(f"slot{r}", [P, HALF_TILES], I32) for r in range(4)]
        r_digits = sb("r_digits", [P, EWORDS, EDIGITS])
        r_words = sb("r_words", [P, EWORDS])
        experts_of = [sb(f"experts_of{r}", [P, EWORDS], I32) for r in range(4)]

        xs = sb("xs", [P, 4, D])
        xT = sb("xT", [P, 2, P])
        w1s = sb("w1s", [P, 2, DFF])
        w2s = sb("w2s", [P, 2, FC, D])
        hT = sb("hT", [P, 2, FC, P])
        ys = sb("ys", [P, 4, D])
        IDS = sb("IDS", [P, (HALF_TILES + FTILES) * ID_RUN], I32)
        token_of = sb("token_of", [P, FTILES, ID_RUN], I32)
        zeros = sb("zeros", [P, D])

        AN = sb("AN", [P, 2, 2, D])
        AT = sb("AT", [P, 2, SEQ])
        QH = sb("QH", [P, 2, 4, SEQ])
        KG = sb("KG", [P, 2, G4, KPAD])
        VB = sb("VB", [P, 2, NQB, P])
        top = sb("top", [P, 2, 16])
        E = sb("E", [P, 2, 16 * 2 * QB])
        PT = sb("PT", [P, 2, (NQB + 1) * 256])
        rden = sb("rden", [P, SEQ])
        ON = sb("ON", [P, SEQ])
        OT = sb("OT", [P, SEQ])

        PS = ctx.enter_context(nc.psum_tensor("PS", [P, 8, 512], F32))
        BANK_ACT, BANK_DVE = 6, 7
        GATE_X_B, GATE_L_B = (BANK_ACT, 0), (BANK_DVE, 1)
        ND = (4, 5)
        XT_B, HA_B, HB_B, Y_B = (0, 1), (2, 3), (4, 5), (6, 7)

        xs_d = [nc.dram_tensor(f"sorted_x{h}", [FTILES * P, D], F32, kind="Internal").ap() for h in range(2)]
        ys_d = [nc.dram_tensor(f"sorted_y{h}", [FTILES * P, D], F32, kind="Internal").ap() for h in range(2)]

        ids_d = nc.dram_tensor("sorted_ids", [FTILES * P, ID_RUN], I32, kind="Internal").ap()
        y_d = nc.dram_tensor("y_by_token", [HALF_TOKENS + FTILES * P, D], F32, kind="Internal").ap()

        x_loaded = [sem(f"x_loaded{g}") for g in range(4)]
        w_gate = sem("w_gate_loaded")
        w_attention = sem("w_attention_loaded")
        w_ffn = sem("w_ffn_loaded")
        b2_halved = sem("b2_halved")
        zeros_ready = sem("zeros_ready")
        pads_zeroed = [sem(f"pads_zeroed{h}") for h in range(2)]
        out_stored = sem("out_stored")
        const_ready = sem("const_ready")
        bufs_zeroed = sem("bufs_zeroed")
        dve_step = sem("dve_step")
        norm_waits = sem("norm_waits")
        pool_step = sem("pool_step")
        mv_ready = sem("mean_var_ready")
        rstd_ready = sem("rstd_ready")
        pool_waits = sem("pool_waits")
        x_mid = sem("x_after_ffn")
        bo_added = sem("bo_added")
        dve_phase = sem("dve_phase")
        act_phase = sem("act_phase")
        gn_ready = sem("gn_ready")
        gx_full = sem("gx_full")
        gt_ready = sem("gt_ready")
        gl_full = sem("gl_full")
        gl_done = sem("gl_done")
        oh_ready = sem("onehot_ready")
        rank_full = sem("rank_full")
        slots_ready = sem("slots_ready")
        route_ready = sem("route_ready")
        scattered = [sem(f"scattered{r}") for r in range(4)]
        gathered = [[sem(f"gathered{r}_{q}") for q in range(4)] for r in range(4)]
        xs_loaded = [sem(f"xs_loaded{s}") for s in range(4)]
        xt_full = sem("ffn_xt_full")
        xt_ready = sem("ffn_xt_ready")
        w2_ready = sem("ffn_w2_ready")
        w1_ready = sem("ffn_w1_ready")
        ha_full = sem("ffn_h_first_full")
        hb_full = sem("ffn_h_second_full")
        ha_ready = sem("ffn_h_first_ready")
        hb_ready = sem("ffn_h_second_ready")
        y_full = sem("ffn_y_full")
        y_ready = sem("ffn_y_ready")
        y_stored = [sem(f"y_stored{s}") for s in range(4)]
        ids_loaded = sem("ids_loaded")
        ids_filled = sem("ids_filled")
        token_of_loaded = sem("token_of_loaded")
        y_scattered = [sem(f"y_scattered{s}") for s in range(4)]
        y_back = [sem(f"y_back{q}") for q in range(4)]
        an_ready = sem("an_ready")
        at_full = sem("at_full")
        at_ready = sem("at_ready")
        qk_full = sem("qk_full")
        qk_ready = sem("qk_ready")
        v_full = sem("v_full")
        v_ready = sem("v_ready")
        s_full = sem("scores_full")
        s_ready = sem("scores_ready")
        e_ready = sem("exp_ready")
        pt_ready = sem("probs_turned")
        pv_full = sem("pv_full")
        on_ready = sem("normalised_ready")
        ot_ready = sem("ot_ready")
        o_full = sem("o_full")
        o_read = sem("o_read")

        N_GATE, N_ATTENTION = 5, 7
        block = ctx.enter_context(nc.Block())

        def done(J):
            return AHEAD + J + 1

        def slot_free(J):
            return AHEAD + J - 1

        ID_SCATTERS = HALF_TILES // 4 * 16

        def transfers(I, s, slots, i):
            return (I * ((FTILES + slots - 1 - s) // slots) + i) * 16

        def store_out(eng, q):
            eng.wait_ge(dve_phase, 5 + q)
            o_t = out.rearrange("b s d -> (b s) d").rearrange("(t p) d -> p t d", p=P)
            eng.dma_start(o_t[:, 4 * q:4 * q + 4, :], X[:, 4 * q:4 * q + 4, :]).then_inc(out_stored, 16)

        @block.sync
        def _(sp):
            x_t = x.rearrange("b s d -> (b s) d").rearrange("(t p) d -> p t d", p=P)
            for q in range(4):
                tiles = slice(q * TILES // 4, (q + 1) * TILES // 4)
                sp.dma_start(X[:, tiles, :], x_t[:, tiles, :]).then_inc(x_loaded[q], 16)
            sp.wait_ge(w_gate, 16 * N_GATE)
            sp.wait_ge(zeros_ready, 1)
            for h in range(2):
                sp.dma_start(xs_d[h].rearrange("(j p) d -> p j d", p=P),
                             zeros[:].unsqueeze(1).broadcast_to([P, FTILES, D])).then_inc(pads_zeroed[h], 16)
            for dst, src in ((WQ, Wq), (WK, Wk), (WV, Wv), (WO, Wo), (BO, bo.partition_broadcast(P))):
                sp.dma_start(dst[:], src).then_inc(w_attention, 16)
            for c, b in ((1, bk), (2, bv)):
                sp.dma_start(BQKV[:, c:c + 1], b.rearrange("(p o) -> p o", o=1)).then_inc(w_attention, 16)
            sp.dma_start(IDS[:], ids).then_inc(ids_loaded, 16)
            sp.dma_start(W1[:], w1.rearrange("e d f -> d e f")).then_inc(w_ffn, 16)
            sp.dma_start(B1[:], b1).then_inc(w_ffn, 16)
            sp.dma_start(B2[:], b2.partition_broadcast(P)).then_inc(w_ffn, 16)
            sp.dma_start(W2[:], w2.rearrange("e (c p) n -> p e c n", p=P)).then_inc(w_ffn, 16)

            def load(I, j, s):
                sp.wait_ge(xt_full, done(I * FTILES + j - 4))
                sp.dma_start(xs[:, s, :], xs_d[I % 2][bass.ds(j * P, P), :]).then_inc(xs_loaded[s], 16)

            sp.wait_ge(ids_loaded, 16)
            sp.dma_start(ids_d.rearrange("(j p) w -> p j w", p=P),
                         IDS[:, HALF_TILES * ID_RUN:].rearrange("p (j w) -> p j w", w=ID_RUN)).then_inc(ids_filled, 16)

            def store(I, j, s):
                if I == 3:
                    return
                sp.wait_ge(y_ready, done(I * FTILES + j))
                sp.dma_start(ys_d[I % 2][bass.ds(j * P, P), :], ys[:, s, :]).then_inc(y_stored[s], 16)

            def begin_ffn(I):
                if I == 2:
                    for q in range(4):
                        sp.wait_ge(gathered[0][q], 64)
                if I == 3:
                    for s in range(4):
                        sp.wait_ge(y_scattered[s], ID_SCATTERS)
                    sp.dma_start(token_of[:], ids_d.rearrange("(j p) w -> p j w", p=P)).then_inc(token_of_loaded, 16)
                sp.wait_ge(scattered[I], 16 * HALF_TILES)
                sp.wait_ge(xt_full, done(I * FTILES - 1))
                for s in range(4):
                    load(I, s, s)

            begin_ffn(0)
            for I in range(4):
                with sp.Fori(0, FLOOPS - 1) as i:
                    for s in range(4):
                        load(I, i * 4 + 4 + s, s)
                        store(I, i * 4 + s, s)
                for j in range(FTILES - FREST - 4, FTILES):
                    if j + 4 < FTILES:
                        load(I, j + 4, j % 4)
                    if j == FTILES - 2 and I in (0, 2):
                        begin_ffn(I + 1)
                    store(I, j, j % 4)
                if I == 1:
                    begin_ffn(2)
            for q in range(4):
                store_out(sp, q)
            for s in range(4):
                sp.wait_ge(y_scattered[s], ID_SCATTERS + transfers(1, s, 4, 0))
            for q in range(4):
                rows = slice(q * 4 * P, (q + 1) * 4 * P)
                sp.dma_start(YG[:, HALF_TILES + 4 * q:HALF_TILES + 4 * q + 4, :],
                             y_d[rows, :].rearrange("(t p) d -> p t d", p=P)).then_inc(y_back[q], 16)
            sp.wait_ge(out_stored, 16 * 8)

        @block.gpsimd
        def _(pool):
            pool.memset(zeros[:], 0.0).then_inc(zeros_ready, 1)
            chain = Chain(pool, pool_step)
            pool.memset(ones_b[:], 1.0)
            pool.memset(eps[:], EPS)
            chain.then(pool.memset(minus_half[:], -0.5))
            pool.memset(VB[:], 0.0)
            pool.memset(KG[:], 0.0).then_inc(bufs_zeroed, 1)

            def spread(k, n):
                return range(HALF_TILES * k // n, HALF_TILES * (k + 1) // n)

            def scatter(I, tiles):
                pool.wait_ge(slots_ready, I + 1)
                pool.wait_ge(gt_ready, AHEAD + gates(I))
                pool.wait_ge(pads_zeroed[I % 2], 16)
                for t in tiles:
                    pool.indirect_dma_start(
                        out=xs_d[I % 2], out_offset=bass.IndirectOffsetOnAxis(ap=slot[I][:, t:t + 1], axis=0),
                        in_=XN[:, (I % 2) * HALF_TILES + t, :], in_offset=None).then_inc(scattered[I], 16)

            def gather(I, tiles):
                for s in range(4):
                    pool.wait_ge(y_stored[s], 16 + transfers(I + 1, s, 4, 0))
                for t in tiles:
                    pool.indirect_dma_start(
                        out=YG[:, (I % 2) * HALF_TILES + t, :], out_offset=None, in_=ys_d[I % 2],
                        in_offset=bass.IndirectOffsetOnAxis(ap=slot[I][:, t:t + 1], axis=0)
                    ).then_inc(gathered[I][t // 4], 16)

            def rsqrt(first, n, norm):
                tiles = slice(first, first + n)
                pool.wait_ge(mv_ready, norm + 1)
                chain.then(pool.tensor_tensor(var_eps[:, tiles], mv[:, tiles, 1], eps[:, tiles], ALU.add))
                return pool.tensor_tensor(rstd[:, tiles], var_eps[:, tiles], minus_half[:, tiles], ALU.pow)

            def normalised(dst, b, k):
                pool.sem_inc(pool_waits, 1)
                chain.then(pool.tensor_tensor(dst, x_of(b), mv[:, k:k + 2, 0:1].broadcast_to([P, 2, D]), ALU.subtract))
                return pool.tensor_tensor(dst, dst, rstd[:, k:k + 2].unsqueeze(2).broadcast_to([P, 2, D]), ALU.mult)

            def x_of(b):
                return X[:, bass.ds(b * 2, 2), :]

            def add_ffn(b):
                pool.tensor_tensor(x_of(b), x_of(b), YG[:, bass.ds(b * 2, 2), :], ALU.add).then_inc(x_mid, 1)

            def step(b, s, have):
                if have(3) and not (isinstance(b, int) and b < 0):
                    add_ffn(b + 3)
                if not have(3) and not have(-1):
                    return
                chain.then(rsqrt(4 * s, 4, b + (2 - FIRST_STEP)))
                if have(-1):
                    pool.wait_ge(gt_ready, AHEAD + GATES0 + b - 2)
                if have(3):
                    wait(pool, at_full, b + 2)
                if have(-1):
                    normalised(GN[:, 1 - s, 0:2], b - 1, 4 * s + 2).then_inc(gn_ready, 1)
                if have(3):
                    normalised(AN[:, 1 - s], b + 3, 4 * s).then_inc(an_ready, 1)
                    pool.wait_ge(an_ready, b + 4)
                    pool.sem_inc(pool_waits, 1)
                    pool.tensor_tensor(x_of(b + 3), x_of(b + 3), BO[:].unsqueeze(1).broadcast_to([P, 2, D]),
                                       ALU.add).then_inc(bo_added, 1)

            for h in range(2):
                rsqrt(h * HALF_TILES, HALF_TILES, h).then_inc(rstd_ready, 1)
            for I in range(2):
                scatter(I, range(HALF_TILES))
            gather(0, range(HALF_TILES))

            pool.wait_ge(w_attention, 16 * N_ATTENTION)

            def before(b):
                for first, I in ((FIRST_STEP, 0), (LOOP[0], 1)):
                    if b == first:
                        for q in range(4):
                            pool.wait_ge(gathered[I][q], 64)
                if b == FIRST_STEP:
                    for first in range(-FIRST_STEP):
                        add_ffn(first)

            def after(b):
                if FFN_STEPS <= b < LOOP[0]:
                    gather(1, spread(b - FFN_STEPS, LOOP[0] - FFN_STEPS))
                if LOOP[1] <= b < BATCH:
                    scatter(2, spread(b - LOOP[1], BATCH - LOOP[1]))

            attention_schedule(pool, step, chain, STEPS_OF_POOL, before, after=after)
            scatter(3, range(HALF_TILES))
            pool.wait_ge(ids_filled, 16)
            for t in range(HALF_TILES):
                pool.indirect_dma_start(
                    out=ids_d, out_offset=bass.IndirectOffsetOnAxis(ap=slot[3][:, t:t + 1], axis=0),
                    in_=IDS[:, t * ID_RUN:(t + 1) * ID_RUN], in_offset=None).then_inc(y_scattered[t % 4], 16)
            pool.wait_ge(token_of_loaded, 16)
            for j in range(FTILES):
                pool.wait_ge(y_ready, done(3 * FTILES + j))
                pool.indirect_dma_start(
                    out=y_d, out_offset=bass.IndirectOffsetOnAxis(ap=token_of[:, j, 0:1], axis=0),
                    in_=ys[:, j % 4, :], in_offset=None).then_inc(y_scattered[j % 4], 16)
                if j < HALF_TILES:
                    gather(2, [j])

        @block.scalar
        def _(act):
            for dst, src in ((C[:], consts), (GW[:], gate_w), (GB[:, 0, :], gate_b.partition_broadcast(P)),
                             (GB[:, 1, :], expert_bias.partition_broadcast(P)),
                             (BQKV[:, 0:1], bq.rearrange("(p o) -> p o", o=1))):
                act.dma_start(dst, src).then_inc(w_gate, 16)
            e = Experts(act, "act")
            for c in (xt_ready, w2_ready, ha_ready, gt_ready):
                act.sem_inc(c, AHEAD)

            def gate_turned(G, s, tile, n, bank):
                act.wait_ge(gn_ready, G + 1)
                nc.scalar.copy(XN[:, bass.ds(tile, n), :], GN[:, s, 0:n, :])
                act.wait_ge(gx_full, G + 1)
                act.wait_ge(gl_full, AHEAD + G - 1)
                nc.scalar.copy(GT[:, s, 0:n * D], PS[:, bank, 0:n * D]).then_inc(gt_ready, 1)

            def ffn(I):
                def xte(j, s):
                    J = I * FTILES + j
                    act.wait_ge(xt_full, done(J))
                    act.wait_ge(hb_full, slot_free(J))
                    nc.scalar.copy(xT[:, s, :], PS[:, XT_B[s], 0:P]).then_inc(xt_ready, 1)

                def relu(j, s, expert):
                    act.wait_ge(ha_full, done(I * FTILES + j))
                    for c in range(FC // 2):
                        last = nc.scalar.activation(hT[:, s, c, :], PS[:, HA_B[s], c * P:(c + 1) * P], ACT.Relu,
                                                    bias=B1[:, bass.ds(expert, 1), c])
                    last.then_inc(ha_ready, 1)

                def place_w2(j, s, expert):
                    J = I * FTILES + j
                    act.wait_ge(y_full, slot_free(J))
                    nc.scalar.mul(w2s[:, s].rearrange("p c n -> p (c n)"),
                                  W2[:, bass.ds(expert, 1), :, :].rearrange("p o c n -> p (o c n)"),
                                  0.5).then_inc(w2_ready, 1)

                act.wait_ge(route_ready, I + 1)
                e.load(experts_of[I])
                xte(0, 0)
                xte(1, 1)
                place_w2(0, 0, e.next(0))
                relu(0, 0, e.next(0))
                with act.Fori(0, FLOOPS) as i:
                    for k in range(4):
                        j, s = i * 4 + k, k % 2
                        xte(j + 2, s)
                        relu(j + 1, 1 - s, e.next(k + 1))
                        place_w2(j + 1, 1 - s, e.next(k + 1))
                        if k == 1:
                            e.move(4)
                    e.passed(4)
                j = FLOOPS * 4
                xte(j + 2, 0)
                place_w2(j + 1, 1, e.next(1))
                relu(j + 1, 1, e.next(1))
                place_w2(j + 2, 0, e.next(2))
                relu(j + 2, 0, e.next(2))
                act.sem_inc(act_phase, 1)

            def at_copy(b, s):
                act.wait_ge(at_full, b + 1)
                wait(act, v_full, b - 1)
                nc.scalar.copy(AT[:, s, :], PS[:, BANK_ACT, 0:SEQ]).then_inc(at_ready, 1)

            def qk_copy(b, s):
                act.wait_ge(qk_full, b + 1)
                wait(act, s_full, 2 * b - 2)
                for h in range(4):
                    nc.scalar.activation(QH[:, s, h, :], PS[:, BANK_ACT, 0:SEQ], ACT.Identity,
                                         bias=BQM[:, h:h + 1], scale=const("head_col")[:, h:h + 1])
                for g in range(G4):
                    r = slice(32 * g, 32 * g + 32)
                    last = nc.scalar.activation(KG[r, s, g, QB:KPAD], PS[r, BANK_ACT, SEQ:2 * SEQ], ACT.Identity,
                                                bias=BQKV[r, 1:2])
                last.then_inc(qk_ready, 1)

            def exp(b, u):
                act.wait_ge(s_ready, 2 * b + u + 1)
                nc.scalar.activation(E[:, u, :], E[:, u, :], ACT.Exp, scale=SCALE).then_inc(e_ready, 1)

            def ot_bias(b):
                act.wait_ge(on_ready, b + 1)
                wait(act, o_full, b)
                nc.scalar.activation(OT[:], ON[:], ACT.Identity, bias=BQKV[:, 2:3]).then_inc(ot_ready, 1)

            def values(b, s):
                act.wait_ge(v_full, b + 1)
                wait(act, pv_full, b - 1)
                for r in range(4):
                    rows = slice(32 * r, 32 * r + 32)
                    last = nc.scalar.copy(
                        VB[rows, s].rearrange("p k (g r j) -> p (k g) r j", r=4, j=HD)[:, :, r, :],
                        PS[rows, BANK_ACT, 2 * D:].rearrange("p (m j) -> p m j", j=HD))
                last.then_inc(v_ready, 1)

            def step(b, s, have):
                if have(0):
                    exp(b, 0)
                if have(-2):
                    gate_turned(GATES0 + b - 2, s, (b - 2) * 2, 2, BANK_ACT)
                if have(1):
                    values(b + 1, 1 - s)
                if have(0):
                    exp(b, 1)
                if have(2):
                    at_copy(b + 2, s)
                if have(-1):
                    ot_bias(b - 1)
                if have(2):
                    qk_copy(b + 2, s)

            act.wait_ge(const_ready, 1)
            act.wait_ge(bufs_zeroed, 1)
            for G in range(GATES0):
                gate_turned(G, G % 2, G * GROUP, GROUP, GATE_X_B[G % 2])
            act.wait_ge(w_ffn, 64)
            nc.scalar.mul(B2[:], B2[:], 0.5).then_inc(b2_halved, 1)
            act.sem_inc(act_phase, 1)
            ffn(0)
            ffn(1)
            act.wait_ge(w_attention, 16 * N_ATTENTION)
            attention_schedule(act, step)
            act.sem_inc(act_phase, 1)
            ffn(2)
            ffn(3)
            for q in range(4, 8):
                store_out(act, q)

        @block.vector
        def _(dve):
            chain = Chain(dve, dve_step)
            e = Experts(dve, "dve")
            for c in (w1_ready, hb_ready, y_ready, gl_done):
                dve.sem_inc(c, AHEAD)
            for s in range(4):
                dve.sem_inc(y_stored[s], 16)

            def prepare_constants():
                def repeated(name, n):
                    return const(name).unsqueeze(1).broadcast_to([P, n, 2 * QB])

                def blocks(mask, at, n):
                    return mask[:, at * 2 * QB:(at + n) * 2 * QB].rearrange("p (m k) -> p m k", k=2 * QB)

                dve.wait_ge(w_gate, 16 * N_GATE)
                nc.vector.tensor_copy(ident_b[:], ident)
                nc.vector.tensor_copy(before_b[:], const("before"))
                nc.vector.tensor_copy(blocks(mask_b, 0, 8), repeated("mask", 8))
                nc.vector.tensor_copy(blocks(mask_first_b, 0, 4), repeated("mask_first", 4))
                nc.vector.tensor_copy(blocks(mask_first_b, 4, 4), repeated("mask", 4))
                nc.vector.tensor_scalar(BQM[:], const("head_col"), BQKV[:, 0:1], None,
                                        ALU.mult).then_inc(const_ready, 1)

            def statistics(k, n):
                dve.sem_inc(norm_waits, 1)
                for t in range(k, k + n):
                    last = nc.vector.bn_aggr(mv[:, t, :], stats[:, t, :])
                return last

            def tile_statistics(tile, k):
                return nc.vector.bn_stats(stats[:, k, :], X[:, bass.ds(tile, 1), :].rearrange("p o d -> p (o d)"))

            def half_statistics(h):
                for t in range(HALF_TILES):
                    tile = h * HALF_TILES + t
                    if tile % (TILES // 4) == 0:
                        dve.wait_ge(x_loaded[tile // (TILES // 4)], 16)
                        dve.sem_inc(norm_waits, 1)
                    last = nc.vector.bn_stats(stats[:, tile, :], X[:, tile, :])
                chain.then(last)
                statistics(h * HALF_TILES, HALF_TILES).then_inc(mv_ready, 1)

            def gate_norm(G):
                dve.wait_ge(gt_ready, AHEAD + G - 1)
                for t in range(GROUP):
                    tile = G * GROUP + t
                    last = nc.vector.tensor_scalar(GN[:, G % 2, t, :], X[:, tile, :], mv[:, tile, 0:1],
                                                   rstd[:, tile:tile + 1], ALU.subtract, ALU.mult)
                last.then_inc(gn_ready, 1)

            def gate_logits(G, tile, n, bank):
                dve.wait_ge(gl_full, AHEAD + G + 1)
                chain.then(nc.vector.tensor_tensor(
                    L0[:, 0:n], PS[:, bank, 2 * D:2 * D + n * EXPERTS].rearrange("p (t e) -> p t e", t=n),
                    GB[:, 0, :].unsqueeze(1).broadcast_to([P, n, EXPERTS]), ALU.add))
                nc.vector.tensor_tensor(L[:, bass.ds(tile, n), :], L0[:, 0:n],
                                        GB[:, 1, :].unsqueeze(1).broadcast_to([P, n, EXPERTS]),
                                        ALU.add).then_inc(gl_done, 1)

            def route(I, meanwhile=lambda: None):
                shape = [P, HALF_TILES, EXPERTS]
                logits = L[:, (I % 2) * HALF_TILES:(I % 2 + 1) * HALF_TILES, :]
                dve.wait_ge(gl_done, AHEAD + gates(I))
                chain.then(nc.vector.tensor_reduce(r_max[:], logits, AX.X, ALU.max))
                chain.then(nc.vector.tensor_tensor(r_a[:], logits, r_max[:].unsqueeze(2).broadcast_to(shape),
                                                   ALU.is_ge))
                chain.then(nc.vector.tensor_tensor(r_b[:], r_a[:], const("rank_down").unsqueeze(1).broadcast_to(shape),
                                                   ALU.mult))
                chain.then(nc.vector.tensor_reduce(r_max[:], r_b[:], AX.X, ALU.max))
                nc.vector.tensor_tensor(onehot[:], r_b[:], r_max[:].unsqueeze(2).broadcast_to(shape),
                                        ALU.is_equal).then_inc(oh_ready, 1)
                meanwhile()
                dve.wait_ge(rank_full, I + 1)
                chain.then(nc.vector.tensor_copy(r_cnt[:], PS[:, BANK_DVE, P:P + EXPERTS]))
                chain.then(nc.vector.tensor_tensor(
                    r_steps[:], r_cnt[:].unsqueeze(2).broadcast_to([P, EXPERTS, HALF_TILES]),
                    const("tile_steps").unsqueeze(1).broadcast_to([P, EXPERTS, HALF_TILES]), ALU.is_gt))
                chain.then(nc.vector.tensor_reduce(r_tiles[:], r_steps[:], AX.X, ALU.add))
                chain.then(nc.vector.tensor_tensor(
                    r_pre[:], r_tiles[:].unsqueeze(1).broadcast_to([P, EXPERTS, EXPERTS]),
                    const("earlier_expert").rearrange("p (e f) -> p e f", e=EXPERTS), ALU.mult))
                chain.then(nc.vector.tensor_reduce(r_first[:], r_pre[:], AX.X, ALU.add))
                chain.then(nc.vector.scalar_tensor_tensor(
                    out=r_a[:], in0=r_first[:].unsqueeze(1).broadcast_to(shape), scalar=float(P),
                    in1=PS[:, BANK_DVE, 0:P].rearrange("p (t e) -> p t e", e=EXPERTS), op0=ALU.mult, op1=ALU.add))
                chain.then(nc.vector.tensor_tensor(r_b[:], r_a[:], onehot[:], ALU.mult))
                chain.then(nc.vector.tensor_reduce(r_slot[:], r_b[:], AX.X, ALU.add))
                nc.vector.tensor_copy(slot[I][:], r_slot[:]).then_inc(slots_ready, 1)
                chain.then(nc.vector.tensor_tensor(r_end[:], r_first[:], r_tiles[:], ALU.add))
                chain.then(nc.vector.tensor_tensor(
                    r_ge[:], const("tile_number").unsqueeze(2).broadcast_to([P, EWORDS * EDIGITS, EXPERTS]),
                    r_end[:].unsqueeze(1).broadcast_to([P, EWORDS * EDIGITS, EXPERTS]), ALU.is_ge))
                chain.then(nc.vector.tensor_reduce(r_et[:], r_ge[:], AX.X, ALU.add))
                chain.then(nc.vector.tensor_scalar(r_et[:], r_et[:], float(EXPERTS - 1), None, ALU.min))
                chain.then(nc.vector.tensor_tensor(
                    r_digits[:], r_et[:].rearrange("p (w k) -> p w k", k=EDIGITS),
                    const("digit").unsqueeze(1).broadcast_to([P, EWORDS, EDIGITS]), ALU.mult))
                chain.then(nc.vector.tensor_reduce(r_words[:], r_digits[:], AX.X, ALU.add))
                nc.vector.tensor_copy(experts_of[I][:], r_words[:]).then_inc(route_ready, 1)

            def place_w1(s, expert):
                nc.vector.tensor_copy(w1s[:, s, :], W1[:, bass.ds(expert, 1), :].rearrange("p o f -> p (o f)")
                                      ).then_inc(w1_ready, 1)

            def begin_ffn(I):
                dve.wait_ge(w_ffn, 64)
                dve.wait_ge(route_ready, I + 1)
                e.load(experts_of[I])
                place_w1(0, e.next(0))
                place_w1(1, e.next(1))

            def ffn(I, before_last=lambda: None):
                def relu(j, s, expert):
                    dve.wait_ge(hb_full, done(I * FTILES + j))
                    for c in range(FC // 2, FC):
                        k = c - FC // 2
                        last = nc.vector.tensor_scalar(hT[:, s, c, :], PS[:, HB_B[s], k * P:(k + 1) * P],
                                                       B1[:, bass.ds(expert, 1), c], 0.0, ALU.add, ALU.max)
                    last.then_inc(hb_ready, 1)

                def add_b2(j, s, i, expert):
                    J = I * FTILES + j
                    dve.wait_ge(y_full, done(J))
                    if I < 3:
                        dve.wait_ge(y_stored[s], 16 + transfers(I, s, 4, i))
                    else:
                        dve.wait_ge(y_scattered[s], ID_SCATTERS + 16 * i)
                    nc.vector.tensor_tensor(ys[:, s, :], PS[:, Y_B[s % 2], 0:D],
                                            B2[:, bass.ds(expert, 1), :].rearrange("p o f -> p (o f)"),
                                            ALU.add).then_inc(y_ready, 1)

                relu(0, 0, e.next(0))
                with dve.Fori(0, FLOOPS) as i:
                    for k in range(4):
                        j, s = i * 4 + k, k % 2
                        place_w1(s, e.next(k + 2))
                        relu(j + 1, 1 - s, e.next(k + 1))
                        add_b2(j, k, i, e.next(k))
                        if k == 1:
                            e.move(4)
                    e.passed(4)
                before_last()
                j = FLOOPS * 4
                place_w1(0, e.next(2))
                relu(j + 1, 1, e.next(1))
                add_b2(j, 0, FLOOPS, e.next(0))
                relu(j + 2, 0, e.next(2))
                add_b2(j + 1, 1, FLOOPS, e.next(1))
                add_b2(j + 2, 2, FLOOPS, e.next(2))

            def add_ffn(tile, n):
                xt = X[:, tile:tile + n, :]
                return nc.vector.tensor_tensor(xt, xt, YG[:, tile:tile + n, :], ALU.add)

            def softmax(b, u):
                sc = PS[:, 2 * u:2 * u + 2, :].rearrange("p k (m n) -> p (k m) n", n=2 * QB)
                dve.wait_ge(s_full, 2 * b + u + 1)
                chain.then(nc.vector.tensor_reduce(top[:, u, :], sc, AX.X, ALU.max))
                nc.vector.tensor_tensor(E[:, u, :].rearrange("p (m n) -> p m n", n=2 * QB), sc,
                                        top[:, u, :].unsqueeze(2).broadcast_to([P, 16, 2 * QB]),
                                        ALU.subtract).then_inc(s_ready, 1)

            def turn(b, s, u):
                dve.wait_ge(e_ready, 2 * b + u + 1)
                wait(dve, pv_full, b - 1)
                at = 4 * u * 256 + QB
                dst = PT[:, s, :]
                dst = bass.AP(dst.tensor, dst.offset + at, [dst.ap[0], [2 * QB, 16], [256 - QB, 2], [1, QB]])
                nc.vector.transpose(dst, E[:, u, :].rearrange("p (m k n) -> p m k n", k=2, n=QB)).then_inc(pt_ready, 1)

            def normalise(b, s):
                dve.wait_ge(pv_full, b + 1)
                chain.then(nc.vector.reciprocal(rden[:], PS[:, ND[s], SEQ:2 * SEQ]))
                wait(dve, ot_ready, b)
                nc.vector.tensor_tensor(ON[:], PS[:, ND[s], 0:SEQ], rden[:], ALU.mult).then_inc(on_ready, 1)

            def residual(b):
                dve.wait_ge(o_full, b + 1)
                dve.wait_ge(bo_added, b + 1)
                xt = X[:, bass.ds(b * 2, 2), :]
                nc.vector.tensor_tensor(xt, xt, PS[:, BANK_DVE, 0:2 * D].rearrange("p (t n) -> p t n", t=2),
                                        ALU.add).then_inc(o_read, 1)

            def step(b, s, have):
                if have(0):
                    softmax(b, 0)
                    softmax(b, 1)
                if have(-1):
                    normalise(b - 1, 1 - s)
                if have(0):
                    turn(b, s, 0)
                if have(3):
                    dve.wait_ge(x_mid, b + 4)
                    dve.sem_inc(norm_waits, 1)
                    for t in range(2):
                        last = tile_statistics((b + 3) * 2 + t, 4 * s + t)
                if have(0):
                    turn(b, s, 1)
                if have(-2):
                    dve.wait_ge(gl_full, AHEAD + GATES0 + b - 1)
                if have(-1):
                    residual(b - 1)
                if have(-2):
                    gate_logits(GATES0 + b - 2, (b - 2) * 2, 2, BANK_DVE)
                if have(-1):
                    dve.wait_ge(o_read, b)
                    dve.sem_inc(norm_waits, 1)
                    for t in range(2):
                        last = tile_statistics((b - 1) * 2 + t, 4 * s + 2 + t)
                if have(3) or have(-1):
                    chain.then(last)
                    wait(dve, an_ready, min(b + 2, BATCH) if isinstance(b, int) else b + 2)
                    if have(-3):
                        dve.wait_ge(gn_ready, GATES0 + b - 2)
                    first, end = 0 if have(3) else 2, 4 if have(-1) else 2
                    statistics(4 * s + first, end - first).then_inc(mv_ready, 1)

            half_statistics(0)
            half_statistics(1)
            prepare_constants()

            def ffn_ahead(I):
                def ahead():
                    dve.sem_inc(dve_phase, 1)
                    begin_ffn(I)
                return ahead

            for h in range(2):
                dve.wait_ge(rstd_ready, h + 1)
                first, end = h * GATES0 // 2, (h + 1) * GATES0 // 2
                gate_norm(first)
                gate_norm(first + 1)
                for G in range(first, end):
                    if G + 2 < end:
                        gate_norm(G + 2)
                    dve.wait_ge(gl_done, AHEAD + G)
                    gate_logits(G, G * GROUP, GROUP, GATE_L_B[G % 2])
                route(h, ffn_ahead(0) if h == 1 else lambda: None)
            dve.wait_ge(b2_halved, 1)
            ffn(0)
            begin_ffn(1)

            def first_norms():
                for b in range(FIRST_STEP, FFN_STEPS):
                    straight_step(step, b)

            ffn(1, first_norms)
            dve.sem_inc(dve_phase, 1)

            def after_loop():
                route(2)
                dve.sem_inc(dve_phase, 1)

            attention_schedule(dve, step, chain, STEPS_OF_DVE, after_loop=after_loop, first=FFN_STEPS)
            route(3, ffn_ahead(2))
            ffn(2)
            begin_ffn(3)
            for s in range(4):
                dve.wait_ge(y_stored[s], 16 + transfers(3, s, 4, 0))

            def first_half():
                for q in range(4):
                    dve.wait_ge(gathered[2][q], 64)
                    add_ffn(4 * q, 4).then_inc(dve_phase, 1)

            ffn(3, first_half)
            for q in range(4):
                dve.wait_ge(y_back[q], 16)
                add_ffn(HALF_TILES + 4 * q, 4).then_inc(dve_phase, 1)

        @block.tensor
        def _(pe):
            for c in (xt_full, ha_full, hb_full, y_full, gl_full):
                pe.sem_inc(c, AHEAD)

            def mm(*a, **k):
                return nc.tensor.matmul(*a, skip_group_check=True, **k)

            def gate_turn(G, s, n, bank):
                pe.wait_ge(gn_ready, G + 1)
                for t in range(n):
                    last = nc.tensor.transpose(PS[:, bank, t * P:(t + 1) * P], GN[:, s, t, :], ident)
                last.then_inc(gx_full, 1)

            def gate_mm(G, s, n, bank):
                pe.wait_ge(gt_ready, AHEAD + G + 1)
                for t in range(n):
                    last = mm(PS[:, bank, 2 * D + t * EXPERTS:2 * D + (t + 1) * EXPERTS], GT[:, s, t * P:(t + 1) * P],
                              GW[:], start=True, stop=True)
                last.then_inc(gl_full, 1)

            def route(I):
                pe.wait_ge(oh_ready, I + 1)
                pe.wait_ge(gl_done, AHEAD + gates(I))
                oh = onehot[:].rearrange("p t e -> p (t e)")
                mm(PS[:, BANK_DVE, 0:P], before_b[:], oh, start=True, stop=False)
                for k in range(1, HALF_TILES):
                    mm(PS[:, BANK_DVE, k * EXPERTS:P], ones_b[:], oh[:, 0:P - k * EXPERTS], start=False, stop=False)
                for k in range(HALF_TILES):
                    last = mm(PS[:, BANK_DVE, P:P + EXPERTS], ones_b[:], oh[:, k * EXPERTS:(k + 1) * EXPERTS],
                              start=False, stop=(k == HALF_TILES - 1))
                last.then_inc(rank_full, 1)

            def ffn(I):
                def turn_x(j, s, i):
                    pe.wait_ge(xs_loaded[s], 16 + transfers(I, s, 4, i))
                    nc.tensor.transpose(PS[:, XT_B[s % 2], 0:P], xs[:, s, :], ident).then_inc(xt_full, 1)

                def up(j, s):
                    J = I * FTILES + j
                    pe.wait_ge(xt_ready, done(J))
                    pe.wait_ge(w1_ready, done(J))
                    for bank, full, half in ((HA_B[s], ha_full, 0), (HB_B[s], hb_full, FC // 2)):
                        for c in range(FC // 2):
                            f = (half + c) * P
                            last = mm(PS[:, bank, c * P:(c + 1) * P], w1s[:, s, f:f + P], xT[:, s, :],
                                      start=True, stop=True)
                        last.then_inc(full, 1)

                def down(j, s):
                    J = I * FTILES + j
                    pe.wait_ge(w2_ready, done(J))
                    pe.wait_ge(ha_ready, done(J))
                    pe.wait_ge(hb_ready, done(J))
                    for c in range(FC):
                        last = mm(PS[:, Y_B[s], 0:D], hT[:, s, c, :], w2s[:, s, c, :],
                                  start=(c == 0), stop=(c == FC - 1))
                    last.then_inc(y_full, 1)

                turn_x(0, 0, 0)
                turn_x(1, 1, 0)
                up(0, 0)
                with pe.Fori(0, FLOOPS) as i:
                    for k in range(4):
                        j, s = i * 4 + k, k % 2
                        turn_x(j + 2, (k + 2) % 4, i + (k + 2) // 4)
                        up(j + 1, 1 - s)
                        down(j, s)
                j = FLOOPS * 4
                turn_x(j + 2, 2, FLOOPS)
                up(j + 1, 1)
                down(j, 0)
                up(j + 2, 0)
                down(j + 1, 1)
                down(j + 2, 0)

            def turn_a(b, s):
                pe.wait_ge(an_ready, b + 1)
                for t in range(2):
                    last = nc.tensor.transpose(PS[:, BANK_ACT, t * P:(t + 1) * P], AN[:, s, t, :], ident)
                last.then_inc(at_full, 1)

            def project_qk(b, s):
                pe.wait_ge(at_ready, b + 1)
                mm(PS[:, BANK_ACT, 0:SEQ], WQ[:], AT[:, s, :], start=True, stop=True)
                mm(PS[:, BANK_ACT, SEQ:2 * SEQ], WK[:], AT[:, s, :], start=True, stop=True).then_inc(qk_full, 1)

            def project_v(b, s):
                pe.wait_ge(at_ready, b + 1)
                for k in range(NQB):
                    for r in range(4):
                        last = mm(PS[32 * r:32 * r + 32, BANK_ACT, 2 * D + k * 32:2 * D + (k + 1) * 32],
                                  AT[:, s, k * QB:(k + 1) * QB],
                                  WV[:].rearrange("p (g r j) -> p g r j", r=4, j=HD)[:, :, r, :],
                                  start=True, stop=True)
                last.then_inc(v_full, 1)

            def scores(b, s, u):
                pe.wait_ge(qk_ready, b + 1)
                wait(pe, s_ready, 2 * b + u - 1)
                for k in range(2):
                    mask = mask_first_b if u == 0 and k == 0 else mask_b
                    mm(PS[:, 2 * u + k, :], ident_b[:], mask[:], start=True, stop=False)
                    for c in range(2):
                        q = QB * (4 * u + 2 * k + c)
                        for h in range(4):
                            last = mm(PS[32 * h:32 * h + 32, 2 * u + k, 256 * c:256 * c + 256],
                                      QH[:, s, h, q:q + QB], KG[:, s, :, q:q + 2 * QB], start=False, stop=True)
                last.then_inc(s_full, 1)

            def weigh(b, s, u):
                pe.wait_ge(pt_ready, 2 * b + u + 1)
                pe.wait_ge(v_ready, b + 1)
                if u == 0:
                    wait(pe, on_ready, b - 1)
                for kb in (range(3) if u == 0 else range(3, NQB)):
                    n = min(2 * QB, SEQ - kb * QB)
                    for g in range(G4):
                        rhs = PT[:, s, (kb + 1) * 256 + g * 64:(kb + 1) * 256 + g * 64 + n]
                        r = slice(32 * g, 32 * g + 32)
                        mm(PS[r, ND[s], kb * QB:kb * QB + n], VB[:, s, kb, r], rhs, start=(kb == 0), stop=False)
                        last = mm(PS[r, ND[s], SEQ + kb * QB:SEQ + kb * QB + n], bd_ones(g), rhs, start=False,
                                  stop=True)
                if u == 1:
                    last.then_inc(pv_full, 1)

            def bd_ones(g):
                return const("head_row_bd")[:, 32 * g:32 * g + 32]

            def project_o(b):
                pe.wait_ge(ot_ready, b + 1)
                for t in range(2):
                    last = mm(PS[:, BANK_DVE, t * D:(t + 1) * D], OT[:, t * P:(t + 1) * P], WO[:],
                              start=True, stop=True)
                last.then_inc(o_full, 1)

            def step(b, s, have):
                if have(-1):
                    weigh(b - 1, 1 - s, 1)
                if have(1) or have(-2):
                    wait(pe, qk_ready, b + 2 if have(1) else BATCH)
                first = isinstance(b, int) and b < 0
                if first and have(1):
                    scores(b + 1, 1 - s, 0)
                if have(1):
                    project_v(b + 1, 1 - s)
                if have(-2):
                    wait(pe, gt_ready, AHEAD + GATES0 + b - 2)
                    gate_turn(GATES0 + b - 2, s, 2, BANK_ACT)
                if have(1) and not first:
                    scores(b + 1, 1 - s, 0)
                if have(2):
                    if have(-2):
                        pe.wait_ge(gt_ready, AHEAD + GATES0 + b - 1)
                    if have(1):
                        pe.wait_ge(v_ready, b + 2)
                    turn_a(b + 2, s)
                if have(1):
                    scores(b + 1, 1 - s, 1)
                if have(-1):
                    wait(pe, o_read, b - 1)
                    wait(pe, gl_done, AHEAD + GATES0 + b - 2)
                    project_o(b - 1)
                if have(-2):
                    if not have(-1):
                        pe.wait_ge(gl_done, AHEAD + GATES0 + b - 2)
                    gate_mm(GATES0 + b - 2, s, 2, BANK_DVE)
                if have(2):
                    project_qk(b + 2, s)
                if have(0):
                    weigh(b, s, 0)

            pe.wait_ge(w_gate, 16 * N_GATE)
            pe.wait_ge(const_ready, 1)
            for h in range(2):
                first, end = h * GATES0 // 2, (h + 1) * GATES0 // 2
                for G in range(first, end + 1):
                    if G < end:
                        pe.wait_ge(gt_ready, AHEAD + G - 1)
                        gate_turn(G, G % 2, GROUP, GATE_X_B[G % 2])
                    if G > first:
                        pe.wait_ge(gl_done, AHEAD + G - 2)
                        gate_mm(G - 1, (G - 1) % 2, GROUP, GATE_L_B[(G - 1) % 2])
                route(h)
            pe.wait_ge(w_ffn, 64)
            pe.wait_ge(act_phase, 1)
            pe.wait_ge(dve_phase, 1)
            ffn(0)
            ffn(1)
            pe.wait_ge(y_ready, done(2 * FTILES - 1))
            pe.wait_ge(act_phase, 3)
            pe.wait_ge(dve_phase, 2)

            def after_loop():
                route(2)
                pe.wait_ge(dve_phase, 3)

            pe.wait_ge(w_attention, 16 * N_ATTENTION)
            attention_schedule(pe, step, after_loop=after_loop)
            pe.wait_ge(gl_done, AHEAD + GATES0 + BATCH)
            route(3)
            pe.wait_ge(act_phase, 4)
            pe.wait_ge(dve_phase, 4)
            ffn(2)
            ffn(3)


FIRST_STEP, LAST_STEP = -3, BATCH + 2
LOOP = (2, BATCH - 4)
FFN_STEPS = -1


def straight_step(step, b):
    step(b, b % 2, lambda k: 0 <= b + k < BATCH)


def attention_schedule(eng, step, chain=None, steps=0, before=lambda b: None, after_loop=lambda: None,
                       after=lambda b: None, first=FIRST_STEP):
    def straight(b):
        before(b)
        straight_step(step, b)
        after(b)

    for b in range(first, LOOP[0]):
        straight(b)
    before(LOOP[0])
    count = (LOOP[1] - LOOP[0]) // 2
    with eng.Fori(0, count) as i:
        if chain:
            chain.enter(i, 2 * steps)
        for s in range(2):
            step(i * 2 + (LOOP[0] + s), s, lambda k: True)
        if chain:
            chain.leave(count)
    after_loop()
    for b in range(LOOP[1], LAST_STEP):
        straight(b)


STEPS_OF_DVE = 5
STEPS_OF_POOL = 4


_INS = ["L0_attn_x", "L0_attn_Wq", "L0_attn_bq", "L0_attn_Wk", "L0_attn_bk", "L0_attn_Wv", "L0_attn_bv",
        "L0_attn_Wo", "L0_attn_bo", "L0_ffn_gate_w", "L0_ffn_gate_b", "L0_ffn_expert_bias", "L0_ffn_w1",
        "L0_ffn_b1", "L0_ffn_w2", "L0_ffn_b2"]


def kernel(**inputs):
    import concourse.bacc as bacc
    from concourse.bass_utils import run_bass_kernel_spmd

    nc = bacc.Bacc("TRN2", target_bir_lowering=False, num_devices=1)
    arrays, args = {}, []
    for name, a in [(n, inputs[n]) for n in _INS] + [("constants", constants()), ("numbers", numbers())]:
        a = np.asarray(a)
        if name == "L0_ffn_gate_w":
            a = a.T
        if name == "L0_ffn_b1":
            a = a.reshape(EXPERTS, FC, P).transpose(2, 0, 1)
        a = np.ascontiguousarray(a)
        arrays[f"in_{name}"] = a
        args.append(nc.dram_tensor(f"in_{name}", a.shape, mybir.dt.from_np(a.dtype), kind="ExternalInput").ap())
    args.append(nc.dram_tensor("out_x", (BATCH, SEQ, D), F32, kind="ExternalOutput").ap())
    macaron(nc, *args)
    r = run_bass_kernel_spmd(nc, [arrays], core_ids=[0])
    return r.results[0]["out_x"]
```
